# Optimizing a Trainium2 kernel written in Bass

```python
import numpy as np
import jax
import jax.numpy as jnp

def _softmax(x, axis=-1):
    return jax.nn.softmax(x, axis=axis)

def _gelu(x):
    return jax.nn.gelu(x, approximate=True)

def _silu(x):
    return jax.nn.silu(x)

def _sigmoid(x):
    return jax.nn.sigmoid(x)

def _layernorm(x, axis=-1, eps=1e-05):
    m = jnp.mean(x, axis=axis, keepdims=True)
    v = jnp.var(x, axis=axis, keepdims=True)
    return (x - m) / jnp.sqrt(v + eps)

def _scatter_add(tgt, idx, src, axis=0):
    return tgt.at[idx].add(src)

def _segment_sum(src, seg, n):
    return jax.ops.segment_sum(src, seg, n)
kernel_name = 'mk_prb_d1_jaxref_r8_ee417d'

def setup_inputs(seed: int=0):
    np.random.seed(seed)
    _w = jnp.asarray

    def _L0_attn_setup():
        import jax, jax.numpy as jnp
        import numpy as np
        import math
        B, T, E, H, DQ, NB, MAXLEN = (4, 128, 128, 16, 64, 10, 128)
        NEG = -1000000000.0

        def _attn_forward(X, Wq, bq, Wk, Wv, Wproj, bproj, Wr, br, b_nd):
            b, t, e = X.shape
            maxlen = b_nd.shape[1]
            nb = b_nd.shape[0]
            h = H
            dq = Wq.shape[1] // h
            Q = (X @ Wq + bq).reshape(b, t, h, dq).transpose(0, 2, 1, 3)
            K = (X @ Wk).reshape(b, t, h, dq).transpose(0, 2, 1, 3)
            V = (X @ Wv).reshape(b, t, h, dq).transpose(0, 2, 1, 3)
            R = (X @ Wr + br).reshape(b, t, h, nb).transpose(0, 2, 1, 3)
            d = jnp.arange(t)[:, None] - jnp.arange(t)[None, :]
            valid = (d >= 0) & (d < maxlen)
            bias = jnp.where(valid, 0.0, NEG).astype(jnp.float32)
            D_ntT = jnp.where(valid[None, :, :], b_nd[:, jnp.clip(d, 0, maxlen - 1)], 0.0)
            extra = jnp.einsum('bhtn,ntp->bhtp', R, D_ntT)
            logits = jnp.einsum('bhtd,bhpd->bhtp', Q, K) / math.sqrt(dq) + bias + extra
            W = jax.nn.softmax(logits, axis=-1)
            A = jnp.einsum('bhtp,bhpd->bhtd', W, V)
            A = A.transpose(0, 2, 1, 3).reshape(b, t, h * dq)
            return A @ Wproj + bproj
        key = jax.random.key(seed)
        k = jax.random.split(key, 10)
        X = jax.random.normal(k[0], (B, T, E), jnp.float32)
        Wq = jax.random.normal(k[1], (E, H * DQ), jnp.float32) * (0.1 / math.sqrt(E))
        bq = jnp.zeros((H * DQ,), jnp.float32)
        Wk = jax.random.normal(k[2], (E, H * DQ), jnp.float32) * (0.2 / math.sqrt(E))
        Wv = jax.random.normal(k[3], (E, H * DQ), jnp.float32) * (1.0 / math.sqrt(E))
        Wproj = jax.random.normal(k[4], (H * DQ, E), jnp.float32) * (1.0 / math.sqrt(H * DQ))
        bproj = jnp.zeros((E,), jnp.float32)
        Wr = jax.random.normal(k[5], (E, H * NB), jnp.float32) * (0.1 / math.sqrt(E))
        br = jnp.zeros((H * NB,), jnp.float32)
        b_nd = jax.random.normal(k[6], (NB, MAXLEN), jnp.float32) * 0.2
        return dict(X=X, Wq=Wq, bq=bq, Wk=Wk, Wv=Wv, Wproj=Wproj, bproj=bproj, Wr=Wr, br=br, b_nd=b_nd)
    _L0_attn_in = _L0_attn_setup()

    def _L0_ffn_setup():
        import jax, jax.numpy as jnp
        import numpy as np
        TOP_K = 2
        key = jax.random.key(seed)
        ks = jax.random.split(key, 6)
        B, T, H, E, F = (2, 256, 128, 8, 512)
        s = 0.02
        return {'hidden_states': jax.random.normal(ks[0], (B, T, H), dtype=jnp.float32), 'router_w': jax.random.normal(ks[1], (E, H), dtype=jnp.float32) * s, 'w1': jax.random.normal(ks[2], (E, F, H), dtype=jnp.float32) * s, 'b1': jax.random.normal(ks[3], (E, F), dtype=jnp.float32) * s, 'w2': jax.random.normal(ks[4], (E, H, F), dtype=jnp.float32) * s, 'b2': jax.random.normal(ks[5], (E, H), dtype=jnp.float32) * s}
    _L0_ffn_in = _L0_ffn_setup()
    _d = {'L0_attn_X': _L0_attn_in['X'], 'L0_attn_Wq': _L0_attn_in['Wq'], 'L0_attn_bq': _L0_attn_in['bq'], 'L0_attn_Wk': _L0_attn_in['Wk'], 'L0_attn_Wv': _L0_attn_in['Wv'], 'L0_attn_Wproj': _L0_attn_in['Wproj'], 'L0_attn_bproj': _L0_attn_in['bproj'], 'L0_attn_Wr': _L0_attn_in['Wr'], 'L0_attn_br': _L0_attn_in['br'], 'L0_attn_b_nd': _L0_attn_in['b_nd'], 'L0_ffn_router_w': _L0_ffn_in['router_w'], 'L0_ffn_w1': _L0_ffn_in['w1'], 'L0_ffn_b1': _L0_ffn_in['b1'], 'L0_ffn_w2': _L0_ffn_in['w2'], 'L0_ffn_b2': _L0_ffn_in['b2']}
    _x0 = _d['L0_attn_X']
    _d['L0_attn_X'] = jax.random.normal(jax.random.fold_in(jax.random.key(seed), 1), (32, 256, 128), dtype=_x0.dtype)
    del _x0
    return _d

def reference(L0_attn_X, L0_attn_Wq, L0_attn_bq, L0_attn_Wk, L0_attn_Wv, L0_attn_Wproj, L0_attn_bproj, L0_attn_Wr, L0_attn_br, L0_attn_b_nd, L0_ffn_router_w, L0_ffn_w1, L0_ffn_b1, L0_ffn_w2, L0_ffn_b2):

    def _L0_attn_ref(X, Wq, bq, Wk, Wv, Wproj, bproj, Wr, br, b_nd):
        import jax, jax.numpy as jnp
        import numpy as np
        import math
        B, T, E, H, DQ, NB, MAXLEN = (4, 128, 128, 16, 64, 10, 128)
        NEG = -1000000000.0

        def _attn_forward(X, Wq, bq, Wk, Wv, Wproj, bproj, Wr, br, b_nd):
            b, t, e = X.shape
            maxlen = b_nd.shape[1]
            nb = b_nd.shape[0]
            h = H
            dq = Wq.shape[1] // h
            Q = (X @ Wq + bq).reshape(b, t, h, dq).transpose(0, 2, 1, 3)
            K = (X @ Wk).reshape(b, t, h, dq).transpose(0, 2, 1, 3)
            V = (X @ Wv).reshape(b, t, h, dq).transpose(0, 2, 1, 3)
            R = (X @ Wr + br).reshape(b, t, h, nb).transpose(0, 2, 1, 3)
            d = jnp.arange(t)[:, None] - jnp.arange(t)[None, :]
            valid = (d >= 0) & (d < maxlen)
            bias = jnp.where(valid, 0.0, NEG).astype(jnp.float32)
            D_ntT = jnp.where(valid[None, :, :], b_nd[:, jnp.clip(d, 0, maxlen - 1)], 0.0)
            extra = jnp.einsum('bhtn,ntp->bhtp', R, D_ntT)
            logits = jnp.einsum('bhtd,bhpd->bhtp', Q, K) / math.sqrt(dq) + bias + extra
            W = jax.nn.softmax(logits, axis=-1)
            A = jnp.einsum('bhtp,bhpd->bhtd', W, V)
            A = A.transpose(0, 2, 1, 3).reshape(b, t, h * dq)
            return A @ Wproj + bproj
        return _attn_forward(X, Wq, bq, Wk, Wv, Wproj, bproj, Wr, br, b_nd)

    def _L0_ffn_ref(hidden_states, router_w, w1, b1, w2, b2):
        import jax, jax.numpy as jnp
        import numpy as np
        TOP_K = 2
        x = hidden_states
        router_logits = jnp.einsum('bth,eh->bte', x, router_w)
        topk_values, topk_indices = jax.lax.top_k(router_logits, TOP_K)
        topk_weights = jax.nn.softmax(topk_values.astype(jnp.float32), axis=-1).astype(x.dtype)
        h1 = jnp.einsum('bth,efh->btef', x, w1) + b1
        h1 = jax.nn.gelu(h1, approximate=False)
        expert_outputs = jnp.einsum('btef,ehf->bteh', h1, w2) + b2
        gather_idx = topk_indices[..., None]
        topk_expert_outputs = jnp.take_along_axis(expert_outputs, gather_idx, axis=2)
        mixed_output = jnp.sum(topk_expert_outputs * topk_weights[..., None], axis=2)
        return mixed_output
    x = L0_attn_X
    xn = _layernorm(x, axis=-1)
    x = x + _L0_attn_ref(xn, L0_attn_Wq, L0_attn_bq, L0_attn_Wk, L0_attn_Wv, L0_attn_Wproj, L0_attn_bproj, L0_attn_Wr, L0_attn_br, L0_attn_b_nd) + _L0_ffn_ref(xn, L0_ffn_router_w, L0_ffn_w1, L0_ffn_b1, L0_ffn_w2, L0_ffn_b2)
    return x

_drawn_inputs = setup_inputs


def setup_inputs(seed=0):
    import zlib

    import numpy as np

    out = dict(_drawn_inputs(seed))
    spreads = {'L0_attn_bq': (0.0, 0.8), 'L0_attn_bproj': (0.0, 0.1), 'L0_attn_br': (0.0, 0.8)}
    factors = {'L0_attn_Wq': 8.0,
     'L0_attn_Wk': 8.0,
     'L0_attn_Wr': 6.967,
     'L0_attn_b_nd': 4.653,
     'L0_ffn_b1': 8.0,
     'L0_ffn_b2': 3.954}
    for name, (base, spread) in spreads.items():
        noise = np.random.default_rng([zlib.crc32(name.encode()), seed]).standard_normal(out[name].shape)
        drawn = base * np.exp(spread * noise) if base else spread * noise
        out[name] = jnp.asarray(drawn.astype(out[name].dtype))
    for name, factor in factors.items():
        out[name] = (out[name] * factor).astype(out[name].dtype)
    return out
```

```python
from contextlib import ExitStack

import concourse.bass as bass
from concourse import mybir

ALU = mybir.AluOpType
ACT = mybir.ActivationFunctionType
AX_X = mybir.AxisListType.X
F32 = mybir.dt.float32
F32R = mybir.dt.float32r

P = 128
BANK = 512
NEG = -1.0e9
BIG = 3.0e38
EPS = 1e-5


def at(start, size):
    return slice(start, start + size) if isinstance(start, int) else bass.ds(start, size)


def wait_from(engine, semaphore, value):
    if not isinstance(value, int) or value > 0:
        engine.wait_ge(semaphore, value)


def wait_apart(engine, semaphore, value, met):
    if isinstance(value, int):
        wait_from(engine, semaphore, value)
    else:
        value = engine.to_reg(value)
        engine.wait_ge(met, 1)
        engine.wait_ge(semaphore, value)


def build(nc, X, Wq, bq, Wk, Wv, Wproj, bproj, Wr, br, b_nd, router_w, w1, b1, w2, b2, out):
    B, T, E = X.shape
    NB, WIN = b_nd.shape
    H = Wr.shape[1] // NB
    DQ = Wq.shape[1] // H
    NX, FF, _ = w1.shape
    TILES = B * T // P
    PAIRS = H // 2
    FC = FF // P
    BLOCKS = B * T // BANK
    PER = BANK // P
    GROUPS = H // PER
    SCALE = 1.0 / float(DQ) ** 0.5
    assert E == P and WIN == P and T == 2 * P and 2 * DQ == P and FC == 4 and NX == 8 and H == 16

    ctx = ExitStack()
    with ctx:
        top = [((nc.sbuf_base + 31) // 32) * 32]

        def sb(name, shape, dt=F32):
            size = 4
            for n in shape[1:]:
                size *= n
            t = nc.alloc_sbuf_tensor_at(name, shape, dt, offset=top[0])
            top[0] += (size + 31) // 32 * 32
            return t

        def sem(name):
            return ctx.enter_context(nc.semaphore(name))

        acc = sb("acc", [P, TILES, E])
        xnT = sb("xnT", [P, B * T])
        wm_hi = sb("wm_hi", [P, H, P], F32R)
        wm_lo = sb("wm_lo", [P, H, P], F32R)
        wg_hi = sb("wg_hi", [P, H * P], F32R)
        wg_lo = sb("wg_lo", [P, H * P], F32R)
        wv_hi = sb("wv_hi", [P, H * DQ], F32R)
        wv_lo = sb("wv_lo", [P, H * DQ], F32R)
        wproj = sb("wproj", [P, PAIRS, E])
        qbias = sb("qbias", [P, 2, PAIRS])
        ident = sb("ident", [P, P])
        wgt = sb("wgt", [P, TILES, NX])
        b1T = sb("b1T", [P, NX * FC])
        b2r = sb("b2r", [NX, E])
        brev = sb("brev", [NB, WIN])
        brT = sb("brT", [NB, H])
        shared = top[0]

        w1_hi = sb("w1_hi", [P, NX * FC, P], F32R)
        w1_lo = sb("w1_lo", [P, NX * FC, P], F32R)
        w2T = sb("w2T", [P, NX, FC, E])
        xb_hi = sb("xb_hi", [P, BANK], F32R)
        xb_lo = sb("xb_lo", [P, BANK], F32R)
        wblk = sb("wblk", [P, PER, NX])
        wbT = sb("wbT", [NX, PER, P])
        hid_at = top[0]
        hid = sb("hid", [P, 2, FC, BANK])
        prep_at = top[0]

        top[0] = hid_at
        stage = sb("stage", [P, NX * FC, P])
        top[0] = prep_at
        wv_r = sb("wv_r", [P, H * DQ])
        wrT = sb("wrT", [NB, H, P])
        lg = sb("lg", [P, TILES, NX])
        lg2 = sb("lg2", [P, TILES, NX])
        hit = sb("hit", [P, TILES, NX])
        one1 = sb("one1", [P, TILES, NX])
        m1 = sb("m1", [P, TILES])
        m2 = sb("m2", [P, TILES])
        r1 = sb("r1", [P, TILES])
        ex = sb("ex", [P, TILES])
        den = sb("den", [P, TILES])
        rank = sb("rank", [P, NX])
        bproj_bc = sb("bproj_bc", [P, E])
        rwT = sb("rwT", [P, NX])
        assert top[0] <= nc.sbuf_usable_end, (top[0], nc.sbuf_usable_end)
        top[0] = shared
        wq_r = sb("wq_r", [P, H * DQ])
        wk_r = sb("wk_r", [P, H * DQ])
        wqT = sb("wqT", [P, PAIRS, P])
        wkT = sb("wkT", [P, PAIRS, P])
        xn = sb("xn", [P, 2, PER, P])
        wr_r = sb("wr_r", [P, H * NB])
        stats = sb("stats", [P, TILES, 6])
        mean = sb("mean", [P, TILES])
        var = sb("var", [P, TILES])
        std = sb("std", [P, TILES])
        rstd = sb("rstd", [P, TILES])
        lgT = sb("lgT", [NX, BANK])
        rw_r = sb("rw_r", [NX, E])
        b_r = sb("b_r", [NB, WIN])
        bT = sb("bT", [P, NB])
        b1_r = sb("b1_r", [NX * FC, P])
        bq_r = sb("bq_r", [PAIRS, P])
        bqT = sb("bqT", [P, PAIRS])
        br_r = sb("br_r", [H, NB])
        flip = sb("flip", [P, P])
        assert top[0] <= shared + 2 * NX * FC * P * 4, top[0] - shared

        top[0] = shared
        extra = sb("extra", [P, H, 3 * P])
        val = sb("val", [P, 2, H * DQ])
        gbias = sb("gbias", [P, H * P])
        br_rep = sb("br_rep", [NB, H, P])
        gst = sb("gst", [P, 2, BANK])
        xg_hi = sb("xg_hi", [P, T], F32R)
        xg_lo = sb("xg_lo", [P, T], F32R)
        xq_hi = sb("xq_hi", [P, T], F32R)
        xq_lo = sb("xq_lo", [P, T], F32R)
        qry = sb("qry", [P, 2, T])
        logit = sb("logit", [P, 2, 3 * P])
        low = sb("low", [P, 2, 2])
        prob = sb("prob", [P, 4, 3 * P])
        total = sb("total", [P, 4, 2])
        inv = sb("inv", [P, 4, 2])
        probT = sb("probT", [P, 4, 3 * P])
        headT = sb("headT", [P, 2, T])
        res = sb("res", [P, 2, E])
        fill = sb("fill", [P, H * P])
        assert top[0] <= nc.sbuf_usable_end, top[0]

        ps = ctx.enter_context(nc.psum_tensor("ps", [P, 8, BANK], F32))

        ROW = 2 * P
        skew = nc.dram_tensor("skew", [2 * H * P * ROW], F32)

        def skew_rows(tile, head, count, first, size, pitch):
            return bass.AP(skew, (tile * H + head) * P * ROW + first,
                           [[pitch, P], [P * ROW, count], [1, size]])

        x_in = [sem(f"x_in{q}") for q in range(4)]
        small_in = sem("small_in")
        w2_in = sem("w2_in")
        w1_in = sem("w1_in")
        attn_in = sem("attn_in")
        const_made = sem("const_made")
        stats_made = sem("stats_made")
        var_ready = sem("var_ready")
        std_ready = sem("std_ready")
        rstd_ready = sem("rstd_ready")
        route_chain = sem("route_chain")
        prep_made = sem("prep_made")
        prep_high = sem("prep_high")
        prep_low = sem("prep_low")
        wv_split = sem("wv_split")
        xn_made = sem("xn_made")
        xnT_psum = sem("xnT_psum")
        xnT_made = sem("xnT_made")
        lgT_psum = sem("lgT_psum")
        lgT_made = sem("lgT_made")
        lg_psum = sem("lg_psum")
        lg_made = sem("lg_made")
        bproj_added = sem("bproj_added")
        route = sem("route")
        route_exp = sem("route_exp")
        block_x = sem("block_x")
        wbT_psum = sem("wbT_psum")
        wbT_made = sem("wbT_made")
        b2_psum = sem("b2_psum")
        b2_added = sem("b2_added")
        hid_psum = sem("hid_psum")
        hid_made = sem("hid_made")
        y_psum = sem("y_psum")
        y_added = sem("y_added")
        fill_made = sem("fill_made")
        filled = sem("filled")
        rep_made = sem("rep_made")
        gb_psum = sem("gb_psum")
        gb_made = sem("gb_made")
        xg_made = sem("xg_made")
        xq_made = sem("xq_made")
        misc_psum = sem("misc_psum")
        val_made = sem("val_made")
        g_staged = sem("g_staged")
        skew_out = [sem(f"skew_out{n}") for n in range(2)]
        skew_in = [sem(f"skew_in{u}") for u in range(2 * GROUPS)]
        q_psum = sem("q_psum")
        q_made = sem("q_made")
        s_psum = sem("s_psum")
        logit_made = sem("logit_made")
        prob_made = sem("prob_made")
        inv_made = sem("inv_made")
        norm_made = sem("norm_made")
        pT_psum = sem("pT_psum")
        pT_made = sem("pT_made")
        head_psum = sem("head_psum")
        head_made = sem("head_made")
        out_psum = sem("out_psum")
        res_made = sem("res_made")
        out_done = sem("out_done")

        PREP = [("w2", NX, False), ("small", 5, False), ("wq", 2, False), ("wk", 2, False), ("wr", 4, False),
                ("brev", 1, False), ("qbias", 2, False), ("wm", 4, True), ("wg", 4, True), ("w1", NX, True)]
        FIRST, SPLITS_BEFORE = {}, []
        n = s = 0
        for name, count, split in PREP:
            FIRST[name] = n
            for _ in range(count):
                SPLITS_BEFORE.append(s)
                s += split
            n += count
        PREP_GROUPS, PREP_SPLITS = n, s
        RING = 4

        XT_BANK, LGT_BANK, LG_BANK = (4, 5), 6, 7
        H_BANK, Y_BANK, WB_BANK, B2_BANK = (0, 1, 2, 3), (4, 5), 6, 7
        Q_BANK, S_BANK, PT_BANK, HEAD_BANK, MISC_BANK, OUT_BANK = (0, 1), (2, 3), 4, 5, 6, 7

        UNITS = [(0, "v", 1, 0), (1, "v", 1, 1), (4, "g", 0, 0), (6, "g", 0, 1), (8, "g", 1, 0), (10, "g", 1, 1),
                 (12, "v", 0, 0), (14, "v", 0, 1), (16, "g", 2, 0), (17, "g", 2, 1), (18, "g", 3, 0), (19, "g", 3, 1)]
        START = [(0, "v", 0, 0), (0, "v", 0, 1)] + [(0, "g", g, t) for g in range(GROUPS) for t in range(2)]
        SLOTS = H + 5
        G_UNITS = 2 * GROUPS

        def wm_heads(w, k):
            a = 8 * (k // 2)
            return w[:, a:a + 8, :].rearrange("p (n two) e -> p two n e", two=2)[:, k % 2, :, :]

        def bank4(g):
            return ps[:, g % RING, :].rearrange("p (n e) -> p n e", n=4)

        block = ctx.enter_context(nc.Block())

        @block.sync
        def _(sp):
            x_v = X.rearrange("b (u p) e -> p (b u) e", p=P)
            sp.dma_start(acc[:, 0:16, :], x_v[:, 0:16, :]).then_inc(x_in[0], 16)
            sp.dma_start(stage[:, :, :].rearrange("p (e c) f -> p e (c f)", e=NX),
                         w2.rearrange("e h f -> h e f")).then_inc(w2_in, 16)
            for q in range(1, 4):
                sp.dma_start(acc[:, 16 * q:16 * q + 16, :], x_v[:, 16 * q:16 * q + 16, :]).then_inc(x_in[q], 16)
            sp.dma_start(rw_r[:, :], router_w).then_inc(small_in, 16)
            sp.dma_start(b_r[:, :], b_nd).then_inc(small_in, 16)
            sp.dma_start(b1_r[:, :], b1.rearrange("e (c f) -> (e c) f", c=FC)).then_inc(small_in, 16)
            sp.dma_start(bq_r[:, :], bq.rearrange("(k d) -> k d", d=P)).then_inc(small_in, 16)
            sp.dma_start(br_r[:, :], br.rearrange("(h n) -> h n", n=NB)).then_inc(small_in, 16)
            sp.dma_start(b2r[:, :], b2).then_inc(small_in, 16)
            sp.dma_start(bproj_bc[:, :], bproj.partition_broadcast(P)).then_inc(small_in, 16)
            sp.dma_start(wq_r[:, :], Wq).then_inc(attn_in, 16)
            sp.dma_start(wk_r[:, :], Wk).then_inc(attn_in, 16)
            sp.dma_start(wr_r[:, :], Wr).then_inc(attn_in, 16)
            sp.dma_start(wv_r[:, :], Wv).then_inc(attn_in, 16)
            sp.dma_start(wproj[:, :, :], Wproj.rearrange("(k d) e -> d k e", d=P)).then_inc(attn_in, 16)
            sp.wait_ge(prep_made, FIRST["small"])
            sp.dma_start(stage[:, :, :], w1.rearrange("e (c f) h -> f (e c) h", c=FC)).then_inc(w1_in, 16)

            sp.wait_ge(fill_made, 1)
            for tile in range(2):
                sp.dma_start(skew_rows(tile, 0, H, P, P, ROW),
                             fill[:, :].rearrange("p (h j) -> p h j", h=H)).then_inc(filled, 16)

            def write_unit(k, g, t):
                wait_apart(sp, g_staged, k + 1, filled)
                sp.dma_start(skew_rows(t, PER * g, PER, 0, P, ROW),
                             gst[:, t, :].rearrange("p (h j) -> p h j", h=PER)
                             ).then_inc(skew_out[t], 16)

            def read_unit(i, g, t):
                wait_apart(sp, skew_out[t], (i * GROUPS + g + 1) * 16, filled)
                wait_apart(sp, logit_made, i * H + PER * (g + 1) - H, filled)
                if t == 0:
                    dst, src = extra[:, PER * g:PER * g + PER, 0:P], skew_rows(0, PER * g, PER, P - 1, P, ROW - 1)
                else:
                    dst, src = extra[:, PER * g:PER * g + PER, P:3 * P], skew_rows(1, PER * g, PER, -1, 2 * P, ROW - 1)
                sp.dma_start(dst, src).then_inc(skew_in[2 * g + t], 16)

            def positions(i, groups):
                last = None
                for g in groups:
                    for t in range(2):
                        wait_apart(sp, skew_in[2 * g + t], i * 16, filled)
                        write_unit(i * G_UNITS + 2 * g + t, g, t)
                        if last:
                            read_unit(i, *last)
                        last = (g, t)
                read_unit(i, *last)

            sp.wait_ge(filled, 32)
            positions(0, range(GROUPS))

            out_v = out.rearrange("b (u p) e -> p (b u) e", p=P)

            def store(i):
                sp.wait_ge(res_made, i + 1)
                sp.dma_start(out_v[:, at(2 * i, 2), :], res[:, :, :]).then_inc(out_done, 16)

            positions(1, range(GROUPS))
            with sp.Fori(1, B - 1) as i:
                positions(i + 1, range(0, 2))
                store(i - 1)
                positions(i + 1, range(2, GROUPS))
            store(B - 2)
            store(B - 1)
            sp.wait_ge(out_done, 16 * B)

        @block.gpsimd
        def _(pool):
            nc.gpsimd.memset(ident[:, :], 0.0).then_inc(const_made, 1)
            nc.gpsimd.memset(flip[:, :], 0.0).then_inc(const_made, 1)
            for e in range(NX):
                nc.gpsimd.memset(rank[:, e:e + 1], float(NX - e)).then_inc(const_made, 1)
            pool.wait_ge(const_made, 2 + NX)
            nc.gpsimd.affine_select(out=ident[:, :], in_=ident[:, :], compare_op=ALU.not_equal, fill=1.0, base=0,
                                    pattern=[[-1, P]], channel_multiplier=1).then_inc(const_made, 1)
            nc.gpsimd.affine_select(out=flip[:, :], in_=flip[:, :], compare_op=ALU.not_equal, fill=1.0, base=1 - P,
                                    pattern=[[1, P]], channel_multiplier=1).then_inc(const_made, 1)
            pool.wait_ge(attn_in, 80)
            nc.gpsimd.tensor_scalar(wv_hi[:, :], wv_r[:, :], 1.0, 1.0, ALU.mult, ALU.mult).then_inc(wv_split, 1)
            pool.wait_ge(wv_split, 1)
            nc.gpsimd.tensor_tensor(wv_lo[:, :], wv_r[:, :], wv_hi[:, :].bitcast(F32), ALU.subtract).then_inc(wv_split, 1)
            pool.wait_ge(small_in, 112)
            with pool.Fori(0, BLOCKS) as k:
                wait_apart(pool, xn_made, k + 1, const_made)
                nc.gpsimd.tensor_tensor(acc[:, at(PER * k, PER), :], acc[:, at(PER * k, PER), :],
                                        bproj_bc[:, :].unsqueeze(1).broadcast_to([P, PER, E]),
                                        ALU.add).then_inc(bproj_added, 1)
            pool.wait_ge(y_added, BLOCKS * NX)
            nc.gpsimd.memset(fill[:, :], -NEG).then_inc(fill_made, 1)

            def split(i, hi, lo, made):
                nc.gpsimd.tensor_copy(hi[:, :], xnT[:, at(i * T, T)]).then_inc(made, 1)
                wait_apart(pool, made, 2 * i + 1, const_made)
                nc.gpsimd.tensor_tensor(lo[:, :], xnT[:, at(i * T, T)], hi[:, :].bitcast(F32),
                                        ALU.subtract).then_inc(made, 1)

            split(0, xg_hi, xg_lo, xg_made)
            split(0, xq_hi, xq_lo, xq_made)

            def sequence(i, last):
                for j in range(SLOTS):
                    if j == 2 and not last:
                        wait_apart(pool, misc_psum, len(START) + i * len(UNITS) + 2, const_made)
                        split(i + 1, xg_hi, xg_lo, xg_made)
                    h = j - 2
                    if 0 <= h < H:
                        wait_apart(pool, inv_made, i * H + h + 1, const_made)
                        nc.gpsimd.tensor_scalar(prob[:, h % 4, 0:P], prob[:, h % 4, 0:P], inv[:, h % 4, 0:1], 1.0,
                                                ALU.mult, ALU.mult).then_inc(norm_made, 1)
                        nc.gpsimd.tensor_scalar(prob[:, h % 4, P:], prob[:, h % 4, P:], inv[:, h % 4, 1:2], 1.0,
                                                ALU.mult, ALU.mult).then_inc(norm_made, 1)
                    if j == H and not last:
                        wait_apart(pool, q_psum, (i + 1) * H, const_made)
                        split(i + 1, xq_hi, xq_lo, xq_made)

            sequence(0, False)
            with pool.Fori(1, B - 1) as i:
                sequence(i, False)
            sequence(B - 1, True)

        @block.scalar
        def _(act):
            def prep_copy(g, dst, src, scale=1.0):
                act.wait_ge(prep_made, g + 1)
                nc.scalar.activation(dst, src, ACT.Copy, scale=scale).then_inc(prep_high, 1)

            def bank(g, parts=P, cols=BANK):
                return ps[0:parts, g % RING, 0:cols]

            g = FIRST["w2"]
            for e in range(NX):
                prep_copy(g + e, w2T[:, e, :, :].rearrange("p c h -> p (c h)"), bank(g + e))
            g = FIRST["small"]
            prep_copy(g, rwT[:, :], bank(g, P, NX))
            prep_copy(g + 1, bT[:, :], bank(g + 1, P, NB))
            prep_copy(g + 2, b1T[:, :], bank(g + 2, P, NX * FC))
            prep_copy(g + 3, bqT[:, :], bank(g + 3, P, PAIRS))
            prep_copy(g + 4, brT[:, :], bank(g + 4, NB, H))
            for w, dst in (("wq", wqT), ("wk", wkT)):
                for k in range(2):
                    prep_copy(FIRST[w] + k, dst[:, 4 * k:4 * k + 4, :].rearrange("p k e -> p (k e)"),
                              bank(FIRST[w] + k))
            for k in range(4):
                prep_copy(FIRST["wr"] + k, wrT[:, 4 * k:4 * k + 4, :].rearrange("p k e -> p (k e)"),
                          bank(FIRST["wr"] + k, NB))
            prep_copy(FIRST["brev"], brev[:, :], bank(FIRST["brev"], NB, WIN), -1.0)
            for k in range(2):
                prep_copy(FIRST["qbias"] + k, qbias[:, k, :], bank(FIRST["qbias"] + k, P, PAIRS), -SCALE)
            for k in range(4):
                prep_copy(FIRST["wm"] + k, wm_heads(wm_hi, k), bank4(FIRST["wm"] + k), -SCALE)
            for k in range(4):
                prep_copy(FIRST["wg"] + k, wg_hi[:, k * BANK:(k + 1) * BANK], bank(FIRST["wg"] + k))

            act.wait_ge(var_ready, 1)
            nc.scalar.activation(std[:, :], var[:, :], ACT.Sqrt).then_inc(std_ready, 1)
            for k in range(2):
                act.wait_ge(xnT_psum, k + 1)
                nc.scalar.copy(xnT[:, k * BANK:(k + 1) * BANK], ps[:, XT_BANK[k % 2], :]).then_inc(xnT_made, 1)
            with act.Fori(1, BLOCKS // 2) as kk:
                for u in range(2):
                    act.wait_ge(xnT_psum, 2 * kk + (u + 1))
                    nc.scalar.copy(xnT[:, at((2 * kk + u) * BANK, BANK)],
                                   ps[:, XT_BANK[u], :]).then_inc(xnT_made, 1)
            for e in range(NX):
                prep_copy(FIRST["w1"] + e, w1_hi[:, FC * e:FC * e + FC, :].rearrange("p c f -> p (c f)"),
                          bank(FIRST["w1"] + e))
            act.wait_ge(route, 1)
            nc.scalar.activation(ex[:, :], m2[:, :], ACT.Exp).then_inc(route_exp, 1)

            def experts(i):
                act.wait_ge(wbT_psum, i + 1)
                nc.scalar.copy(wbT[:, :, :].rearrange("e t p -> e (t p)"),
                               ps[0:NX, WB_BANK, :]).then_inc(wbT_made, 1)
                for e in range(NX):
                    for c in range(FC):
                        act.wait_ge(hid_psum, i * (NX * FC) + (FC * e + c + 1))
                        if c == 0:
                            wait_from(act, y_psum, i * NX + e - 1)
                        nc.scalar.activation(hid[:, e % 2, c, :], ps[:, H_BANK[c], :], ACT.Gelu,
                                             bias=b1T[:, FC * e + c:FC * e + c + 1]).then_inc(hid_made, 1)

            experts(0)
            with act.Fori(1, BLOCKS) as i:
                experts(i)

            for k in range(GROUPS):
                act.wait_ge(gb_psum, k + 1)
                nc.scalar.copy(gbias[:, k * BANK:(k + 1) * BANK], ps[:, k % 4, :]).then_inc(gb_made, 1)

            def values(count, half, tile):
                act.wait_ge(misc_psum, count + 1)
                nc.scalar.copy(val[:, tile, half * BANK:(half + 1) * BANK], ps[:, MISC_BANK, :]).then_inc(val_made, 1)

            for n, (_, kind, half, tile) in enumerate(START):
                if kind == "v":
                    values(n, half, tile)

            def sequence(i, last):
                for j in range(SLOTS):
                    if j < H:
                        act.wait_ge(q_psum, i * H + j + 1)
                        wait_from(act, s_psum, i * H + j - 1)
                        nc.scalar.activation(qry[:, j % 2, :], ps[:, Q_BANK[j % 2], 0:T], ACT.Identity,
                                             bias=qbias[:, j % 2, j // 2:j // 2 + 1]).then_inc(q_made, 1)
                    for n, (slot, kind, half, tile) in enumerate(UNITS):
                        if slot == j and kind == "v" and not (last and n >= 2):
                            if half == 1:
                                wait_from(act, head_psum, i * PAIRS)
                            else:
                                act.wait_ge(head_psum, i * PAIRS + PAIRS // 2)
                            values(len(START) + i * len(UNITS) + n, half, tile)
                    h = j - 1
                    if 0 <= h < H:
                        act.wait_ge(logit_made, i * H + h + 1)
                        wait_from(act, pT_psum, i * H + h - 3)
                        for t, (a, b) in enumerate(((0, P), (P, 3 * P))):
                            nc.scalar.activation(prob[:, h % 4, a:b], logit[:, h % 2, a:b], ACT.Exp, scale=-1.0,
                                                 bias=low[:, h % 2, t:t + 1],
                                                 accum_out=total[:, h % 4, t:t + 1]).then_inc(prob_made, 1)
                    h = j - 4
                    if h > 0 and h % 2:
                        pair = h // 2
                        act.wait_ge(head_psum, i * PAIRS + pair + 1)
                        wait_from(act, out_psum, i * PAIRS + pair - 1)
                        nc.scalar.copy(headT[:, pair % 2, :], ps[:, HEAD_BANK, 0:T]).then_inc(head_made, 1)

            sequence(0, False)
            with act.Fori(1, B - 1) as i:
                sequence(i, False)
            sequence(B - 1, True)

        @block.vector
        def _(dve):
            chain = [0]

            def link(ins):
                chain[0] += 1
                ins.then_inc(route_chain, 1)
                dve.wait_ge(route_chain, chain[0])

            GRP = 8
            for q in range(4):
                dve.wait_ge(x_in[q], 16)
                with dve.Fori(2 * q, 2 * q + 2) as s:
                    for n in range(GRP):
                        ins = nc.vector.bn_stats(stats[:, at(GRP * s + n, 1), :].rearrange("p a b -> p (a b)"),
                                                 acc[:, at(GRP * s + n, 1), :].rearrange("p a b -> p (a b)"))
                    ins.then_inc(stats_made, 1)
            dve.wait_ge(stats_made, TILES // GRP)
            mean_e, dev_e, mean_o, dev_o = (stats[:, :, n] for n in (1, 2, 4, 5))
            link(nc.vector.tensor_tensor(mean[:, :], mean_e, mean_o, ALU.add))
            link(nc.vector.tensor_scalar(mean[:, :], mean[:, :], 0.5, None, ALU.mult))
            link(nc.vector.tensor_tensor(std[:, :], mean_e, mean_o, ALU.subtract))
            link(nc.vector.scalar_tensor_tensor(out=std[:, :], in0=std[:, :], scalar=0.25, in1=std[:, :],
                                                op0=ALU.mult, op1=ALU.mult))
            link(nc.vector.tensor_tensor(var[:, :], dev_e, dev_o, ALU.add))
            link(nc.vector.scalar_tensor_tensor(out=var[:, :], in0=var[:, :], scalar=1.0 / E, in1=std[:, :],
                                                op0=ALU.mult, op1=ALU.add))
            nc.vector.tensor_scalar(var[:, :], var[:, :], EPS, None, ALU.add).then_inc(var_ready, 1)

            def low_part(g, dst, hi, src, scale):
                dve.wait_ge(prep_high, g + 1)
                nc.vector.scalar_tensor_tensor(out=dst, in0=src, scalar=scale, in1=hi, op0=ALU.mult,
                                               op1=ALU.subtract).then_inc(prep_low, 1)

            for k in range(4):
                g = FIRST["wm"] + k
                low_part(g, wm_heads(wm_lo, k), wm_heads(wm_hi, k).bitcast(F32), bank4(g), -SCALE)
            for k in range(4):
                g = FIRST["wg"] + k
                low_part(g, wg_lo[:, k * BANK:(k + 1) * BANK],
                         wg_hi[:, k * BANK:(k + 1) * BANK].bitcast(F32), ps[:, g % RING, :], 1.0)
            dve.wait_ge(std_ready, 1)
            nc.vector.reciprocal(rstd[:, :], std[:, :]).then_inc(rstd_ready, 1)
            dve.wait_ge(rstd_ready, 1)

            def norm_block(k, u):
                wait_from(dve, xnT_psum, k - 1)
                for n in range(PER):
                    ins = nc.vector.tensor_scalar(
                        xn[:, u, n, :], acc[:, at(PER * k + n, 1), :].rearrange("p a b -> p (a b)"),
                        mean[:, at(PER * k + n, 1)], rstd[:, at(PER * k + n, 1)],
                        ALU.subtract, ALU.mult)
                ins.then_inc(xn_made, 1)

            def logits_T(k):
                dve.wait_ge(lgT_psum, k + 1)
                wait_from(dve, lg_psum, k)
                nc.vector.tensor_copy(lgT[:, :], ps[0:NX, LGT_BANK, :]).then_inc(lgT_made, 1)

            def logits(k):
                dve.wait_ge(lg_psum, k + 1)
                nc.vector.tensor_copy(lg[:, at(PER * k, PER), :],
                                      ps[:, LG_BANK, 0:PER * NX].rearrange("p (t e) -> p t e", t=PER)
                                      ).then_inc(lg_made, 1)

            norm_block(0, 0)
            norm_block(1, 1)
            logits_T(0)
            with dve.Fori(1, BLOCKS // 2) as kk:
                for u in range(2):
                    norm_block(2 * kk + u, u)
                    logits(2 * kk + (u - 2))
                    logits_T(2 * kk + (u - 1))
            logits(BLOCKS - 2)
            logits_T(BLOCKS - 1)
            logits(BLOCKS - 1)

            for e in range(NX):
                g = FIRST["w1"] + e
                low_part(g, w1_lo[:, FC * e:FC * e + FC, :].rearrange("p c f -> p (c f)"),
                         w1_hi[:, FC * e:FC * e + FC, :].rearrange("p c f -> p (c f)").bitcast(F32),
                         ps[:, g % RING, :], 1.0)

            wide = [P, TILES, NX]
            ranks = rank[:, :].unsqueeze(1).broadcast_to(wide)

            def over(v):
                return v[:, :].unsqueeze(2).broadcast_to(wide)

            dve.wait_ge(lg_made, BLOCKS)
            dve.wait_ge(const_made, 2 + NX)
            link(nc.vector.tensor_reduce(m1[:, :], lg[:, :, :], AX_X, ALU.max))
            link(nc.vector.tensor_tensor(hit[:, :, :], lg[:, :, :], over(m1), ALU.is_equal))
            link(nc.vector.tensor_tensor(hit[:, :, :], hit[:, :, :], ranks, ALU.mult))
            link(nc.vector.tensor_reduce(r1[:, :], hit[:, :, :], AX_X, ALU.max))
            link(nc.vector.tensor_tensor(one1[:, :, :], hit[:, :, :], over(r1), ALU.is_equal))
            link(nc.vector.scalar_tensor_tensor(out=lg2[:, :, :], in0=one1[:, :, :], scalar=-BIG, in1=lg[:, :, :],
                                                op0=ALU.mult, op1=ALU.add))
            link(nc.vector.tensor_reduce(m2[:, :], lg2[:, :, :], AX_X, ALU.max))
            link(nc.vector.tensor_tensor(hit[:, :, :], lg2[:, :, :], over(m2), ALU.is_equal))
            link(nc.vector.tensor_tensor(hit[:, :, :], hit[:, :, :], ranks, ALU.mult))
            link(nc.vector.tensor_reduce(r1[:, :], hit[:, :, :], AX_X, ALU.max))
            link(nc.vector.tensor_tensor(hit[:, :, :], hit[:, :, :], over(r1), ALU.is_equal))
            nc.vector.tensor_tensor(m2[:, :], m2[:, :], m1[:, :], ALU.subtract).then_inc(route, 1)
            dve.wait_ge(route_exp, 1)
            link(nc.vector.tensor_scalar(den[:, :], ex[:, :], 1.0, None, ALU.add))
            link(nc.vector.reciprocal(m1[:, :], den[:, :]))
            link(nc.vector.tensor_tensor(m2[:, :], ex[:, :], m1[:, :], ALU.mult))
            link(nc.vector.tensor_tensor(one1[:, :, :], one1[:, :, :], over(m1), ALU.mult))
            link(nc.vector.tensor_tensor(hit[:, :, :], hit[:, :, :], over(m2), ALU.mult))
            link(nc.vector.tensor_tensor(wgt[:, :, :], one1[:, :, :], hit[:, :, :], ALU.add))
            dve.wait_ge(bproj_added, BLOCKS)

            def block_in(i):
                wait_from(dve, hid_psum, i * (NX * FC))
                x_blk = xnT[:, at(i * BANK, BANK)]
                nc.vector.tensor_copy(xb_hi[:, :], x_blk).then_inc(block_x, 1)
                nc.vector.tensor_copy(wblk[:, :, :], wgt[:, at(PER * i, PER), :]).then_inc(block_x, 1)
                dve.wait_ge(block_x, 3 * i + 1)
                nc.vector.tensor_tensor(xb_lo[:, :], x_blk, xb_hi[:, :].bitcast(F32), ALU.subtract).then_inc(block_x, 1)

            def experts(i, last):
                dve.wait_ge(b2_psum, i + 1)
                a = acc[:, at(PER * i, PER), :]
                nc.vector.tensor_tensor(a, ps[:, B2_BANK, :].rearrange("p (t e) -> p t e", t=PER), a,
                                        ALU.add).then_inc(b2_added, 1)
                dve.wait_ge(b2_added, i + 1)
                for e in range(NX):
                    if e == NX - 1 and not last:
                        block_in(i + 1)
                    dve.wait_ge(y_psum, i * NX + e + 1)
                    if e:
                        dve.wait_ge(y_added, i * NX + e)
                    for t in range(PER):
                        a = acc[:, at(PER * i + t, 1), :].rearrange("p a b -> p (a b)")
                        ins = nc.vector.scalar_tensor_tensor(out=a, in0=ps[:, Y_BANK[e % 2], t * P:(t + 1) * P],
                                                             scalar=wgt[:, at(PER * i + t, 1), e], in1=a,
                                                             op0=ALU.mult, op1=ALU.add)
                    ins.then_inc(y_added, 1)

            block_in(0)
            experts(0, False)
            with dve.Fori(1, BLOCKS - 1) as i:
                experts(i, False)
            experts(BLOCKS - 1, True)
            dve.wait_ge(y_added, BLOCKS * NX)

            nc.vector.tensor_copy(br_rep[:, :, :], brT[:, :].unsqueeze(2).broadcast_to([NB, H, P])).then_inc(rep_made, 1)

            def positions(count, k, g, t):
                i, u = k
                dve.wait_ge(misc_psum, count + 1)
                wait_from(dve, skew_out[t], (i * GROUPS + g) * 16)
                nc.vector.tensor_tensor(gst[:, t, :], ps[:, MISC_BANK, :], gbias[:, g * BANK:(g + 1) * BANK],
                                        ALU.add).then_inc(g_staged, 1)

            dve.wait_ge(gb_made, GROUPS)
            for n, (_, kind, g, t) in enumerate(START):
                if kind == "g":
                    positions(n, (0, 2 * g + t), g, t)

            def sequence(i, last):
                for j in range(SLOTS):
                    h = j - 2
                    if 0 <= h < H:
                        dve.wait_ge(prob_made, 2 * (i * H + h + 1))
                        wait_from(dve, norm_made, 2 * (i * H + h - 3))
                        nc.vector.reciprocal(inv[:, h % 4, :], total[:, h % 4, :]).then_inc(inv_made, 1)
                    h = j - 1
                    if 0 <= h < H:
                        wait_apart(dve, s_psum, i * H + h + 1, const_made)
                        wait_apart(dve, prob_made, 2 * (i * H + h - 1), const_made)
                        if h % PER == 0:
                            wait_apart(dve, skew_in[2 * (h // PER)], (i + 1) * 16, const_made)
                            dve.wait_ge(skew_in[2 * (h // PER) + 1], (i + 1) * 16)
                        for t, (a, b) in enumerate(((0, P), (P, 3 * P))):
                            ins = nc.vector.tensor_tensor_reduce(
                                out=logit[:, h % 2, a:b], in0=ps[:, S_BANK[h % 2], a:b], in1=extra[:, h, a:b],
                                scale=1.0, scalar=BIG, op0=ALU.add, op1=ALU.min, accum_out=low[:, h % 2, t:t + 1])
                        ins.then_inc(logit_made, 1)
                    h = j - 3
                    if 0 <= h < H:
                        dve.wait_ge(pT_psum, i * H + h + 1)
                        wait_from(dve, head_psum, i * PAIRS + h // 2 - 1)
                        nc.vector.tensor_copy(probT[:, h % 4, :], ps[:, PT_BANK, 0:3 * P]).then_inc(pT_made, 1)
                    for n, (slot, kind, g, t) in enumerate(UNITS):
                        if slot == j and kind == "g" and not last:
                            positions(len(START) + i * len(UNITS) + n, (i + 1, 2 * g + t), g, t)
                dve.wait_ge(out_psum, (i + 1) * PAIRS)
                wait_from(dve, out_done, i * 16)
                nc.vector.tensor_tensor(res[:, :, :], ps[:, OUT_BANK, 0:2 * E].rearrange("p (t e) -> p t e", t=2),
                                        acc[:, at(2 * i, 2), :], ALU.add).then_inc(res_made, 1)

            sequence(0, False)
            with dve.Fori(1, B - 1) as i:
                sequence(i, False)
            sequence(B - 1, True)

        @block.tensor
        def _(pe):
            def room(g):
                if g >= RING:
                    pe.wait_ge(prep_high, g - RING + 1)
                    done = SPLITS_BEFORE[g - RING + 1]
                    if done:
                        pe.wait_ge(prep_low, done)
                return g % RING

            pe.wait_ge(const_made, 4 + NX)
            pe.wait_ge(w2_in, 16)
            for e in range(NX):
                b = room(FIRST["w2"] + e)
                for c in range(FC):
                    mm = nc.tensor.transpose(ps[:, b, c * P:(c + 1) * P], stage[:, FC * e + c, :], ident[:, :])
                mm.then_inc(prep_made, 1)
            pe.wait_ge(small_in, 112)
            for k, (src, rows, cols) in enumerate(((rw_r, NX, E), (b_r, NB, WIN), (b1_r, NX * FC, P), (bq_r, PAIRS, P),
                                                   (br_r, H, NB))):
                b = room(FIRST["small"] + k)
                nc.tensor.transpose(ps[0:cols, b, 0:rows], src[:, :], ident[0:rows, 0:rows]).then_inc(prep_made, 1)
            pe.wait_ge(attn_in, 80)
            for w, src in (("wq", wq_r), ("wk", wk_r)):
                for k in range(2):
                    b = room(FIRST[w] + k)
                    for n in range(4):
                        mm = nc.tensor.transpose(ps[:, b, n * P:(n + 1) * P], src[:, (4 * k + n) * P:(4 * k + n + 1) * P],
                                                 ident[:, :])
                    mm.then_inc(prep_made, 1)
            for k in range(4):
                b = room(FIRST["wr"] + k)
                for n in range(4):
                    h = 4 * k + n
                    mm = nc.tensor.transpose(ps[0:NB, b, n * P:(n + 1) * P], wr_r[:, h * NB:(h + 1) * NB], ident[:, :])
                mm.then_inc(prep_made, 1)
            b = room(FIRST["brev"])
            pe.wait_ge(prep_high, FIRST["small"] + 2)
            nc.tensor.matmul(ps[0:NB, b, 0:WIN], bT[:, :], flip[:, :], start=True, stop=True).then_inc(prep_made, 1)
            for k in range(2):
                b = room(FIRST["qbias"] + k)
                pe.wait_ge(prep_high, FIRST["wr"])
                for n in range(PAIRS):
                    rows = slice(DQ * k, DQ * k + DQ)
                    mm = nc.tensor.matmul(ps[:, b, n:n + 1], wkT[rows, n, :], bqT[rows, n:n + 1], start=True, stop=True)
                mm.then_inc(prep_made, 1)

            for k in range(4):
                b = room(FIRST["wm"] + k)
                pe.wait_ge(prep_high, FIRST["wr"])
                for n in range(4):
                    pair = 4 * (k // 2) + n
                    rows = slice(DQ * (k % 2), DQ * (k % 2) + DQ)
                    mm = nc.tensor.matmul(ps[:, b, n * P:(n + 1) * P], wqT[rows, pair, :], wkT[rows, pair, :],
                                          start=True, stop=True)
                mm.then_inc(prep_made, 1)
            for k in range(4):
                b = room(FIRST["wg"] + k)
                pe.wait_ge(prep_high, FIRST["brev"] + 1)
                for n in range(4):
                    mm = nc.tensor.matmul(ps[:, b, n * P:(n + 1) * P], wrT[:, 4 * k + n, :], brev[:, :],
                                          start=True, stop=True)
                mm.then_inc(prep_made, 1)

            def turn(k, u):
                pe.wait_ge(xn_made, k + 1)
                wait_from(pe, xnT_made, k - 1)
                for n in range(PER):
                    mm = nc.tensor.transpose(ps[:, XT_BANK[u], n * P:(n + 1) * P], xn[:, u, n, :], ident[:, :])
                mm.then_inc(xnT_psum, 1)

            def router(k):
                pe.wait_ge(xnT_made, k + 1)
                wait_from(pe, lgT_made, k)
                nc.tensor.matmul(ps[0:NX, LGT_BANK, :], rwT[:, :], xnT[:, at(k * BANK, BANK)],
                                 start=True, stop=True).then_inc(lgT_psum, 1)

            def router_back(k):
                wait_apart(pe, lgT_made, k + 1, const_made)
                wait_apart(pe, lg_made, k, const_made)
                for n in range(PER):
                    mm = nc.tensor.transpose(ps[:, LG_BANK, n * NX:(n + 1) * NX], lgT[:, n * P:(n + 1) * P],
                                             ident[0:NX, 0:NX])
                mm.then_inc(lg_psum, 1)

            pe.wait_ge(prep_high, FIRST["small"] + 1)
            turn(0, 0)
            turn(1, 1)
            router(0)
            with pe.Fori(1, BLOCKS // 2) as kk:
                for u in range(2):
                    router_back(2 * kk + (u - 2))
                    turn(2 * kk + u, u)
                    router(2 * kk + (u - 1))
            router_back(BLOCKS - 2)
            router(BLOCKS - 1)
            router_back(BLOCKS - 1)

            pe.wait_ge(w1_in, 16)
            for e in range(NX):
                b = room(FIRST["w1"] + e)
                for c in range(FC):
                    mm = nc.tensor.transpose(ps[:, b, c * P:(c + 1) * P], stage[:, FC * e + c, :], ident[:, :])
                mm.then_inc(prep_made, 1)
            pe.wait_ge(prep_high, PREP_GROUPS)
            pe.wait_ge(prep_low, PREP_SPLITS)

            def product(dst, parts, start=True, stop=True):
                (a_hi, a_lo), (b_hi, b_lo) = parts
                nc.tensor.matmul(dst, a_hi, b_hi, start=start, stop=False)
                nc.tensor.matmul(dst, a_hi, b_lo, start=False, stop=False)
                return nc.tensor.matmul(dst, a_lo, b_hi, start=False, stop=stop)

            def expert_in(i, e):
                for c in range(FC):
                    wait_from(pe, hid_made, i * (NX * FC) + FC * e + c - FC + 1)
                    product(ps[:, H_BANK[c], :], ((w1_hi[:, FC * e + c, :], w1_lo[:, FC * e + c, :]),
                                                  (xb_hi[:, :], xb_lo[:, :]))).then_inc(hid_psum, 1)

            def expert_out(i, e):
                pe.wait_ge(hid_made, i * (NX * FC) + FC * (e + 1))
                wait_from(pe, y_added, i * NX + e - 1)
                for t in range(PER):
                    for c in range(FC):
                        mm = nc.tensor.matmul(ps[:, Y_BANK[e % 2], t * P:(t + 1) * P],
                                              hid[:, e % 2, c, t * P:(t + 1) * P], w2T[:, e, c, :],
                                              start=(c == 0), stop=(c == FC - 1))
                mm.then_inc(y_psum, 1)

            def experts(i):
                pe.wait_ge(block_x, 3 * i + 3)
                for t in range(PER):
                    mm = nc.tensor.transpose(ps[0:NX, WB_BANK, t * P:(t + 1) * P], wblk[:, t, :], ident[:, :])
                mm.then_inc(wbT_psum, 1)
                expert_in(i, 0)
                pe.wait_ge(wbT_made, i + 1)
                wait_from(pe, b2_added, i)
                for t in range(PER):
                    mm = nc.tensor.matmul(ps[:, B2_BANK, t * P:(t + 1) * P], wbT[:, t, :], b2r[:, :],
                                          start=True, stop=True)
                mm.then_inc(b2_psum, 1)
                for e in range(1, NX):
                    expert_in(i, e)
                    expert_out(i, e - 1)
                expert_out(i, NX - 1)

            experts(0)
            with pe.Fori(1, BLOCKS) as i:
                experts(i)

            pe.wait_ge(rep_made, 1)
            for k in range(GROUPS):
                for n in range(PER):
                    mm = nc.tensor.matmul(ps[:, k % 4, n * P:(n + 1) * P], br_rep[:, PER * k + n, :], brev[:, :],
                                          start=True, stop=True)
                mm.then_inc(gb_psum, 1)
            pe.wait_ge(gb_made, GROUPS)
            pe.wait_ge(wv_split, 2)

            def unit(count, gs, kind, n, tile):
                vs, gg = gs
                wait_from(pe, val_made, vs)
                wait_from(pe, g_staged, gg)
                w_hi, w_lo = (wg_hi, wg_lo) if kind == "g" else (wv_hi, wv_lo)
                rows, cols = slice(tile * P, (tile + 1) * P), slice(n * BANK, (n + 1) * BANK)
                product(ps[:, MISC_BANK, :], ((xg_hi[:, rows], xg_lo[:, rows]),
                                              (w_hi[:, cols], w_lo[:, cols]))).then_inc(misc_psum, 1)

            pe.wait_ge(xg_made, 2)
            vs = gg = 0
            for n, (_, kind, k, t) in enumerate(START):
                unit(n, (vs, gg), kind, k, t)
                vs, gg = vs + (kind == "v"), gg + (kind == "g")

            def sequence(i, last):
                v_before, g_before = 2, G_UNITS
                for j in range(SLOTS):
                    if j < H:
                        if j == 0:
                            pe.wait_ge(xq_made, 2 * i + 2)
                        wait_from(pe, q_made, i * H + j - 1)
                        product(ps[:, Q_BANK[j % 2], 0:T], ((wm_hi[:, j, :], wm_lo[:, j, :]),
                                                            (xq_hi[:, :], xq_lo[:, :]))).then_inc(q_psum, 1)
                    for n, (slot, kind, k, t) in enumerate(UNITS):
                        if slot == j and not (last and n >= 2):
                            if n == 2:
                                pe.wait_ge(xg_made, 2 * i + 4)
                            unit(0, (i * 4 + v_before, i * G_UNITS + g_before), kind, k, t)
                            v_before, g_before = v_before + (kind == "v"), g_before + (kind == "g")
                    h = j - 1
                    if 0 <= h < H:
                        pe.wait_ge(q_made, i * H + h + 1)
                        wait_from(pe, logit_made, i * H + h - 1)
                        nc.tensor.matmul(ps[:, S_BANK[h % 2], 0:P], qry[:, h % 2, 0:P], xnT[:, at(i * T, P)],
                                         start=True, stop=True)
                        nc.tensor.matmul(ps[:, S_BANK[h % 2], P:3 * P], qry[:, h % 2, P:T], xnT[:, at(i * T, T)],
                                         start=True, stop=True).then_inc(s_psum, 1)
                    h = j - 3
                    if 0 <= h < H:
                        pe.wait_ge(norm_made, 2 * (i * H + h + 1))
                        wait_from(pe, pT_made, i * H + h)
                        for n, src in enumerate((0, 1, 2)):
                            mm = nc.tensor.transpose(ps[:, PT_BANK, n * P:(n + 1) * P],
                                                     prob[:, h % 4, src * P:(src + 1) * P], ident[:, :])
                        mm.then_inc(pT_psum, 1)
                    h = j - 4
                    if h > 0 and h % 2:
                        pair = h // 2
                        if pair == 0:
                            pe.wait_ge(val_made, 4 * i + 2)
                        if pair == PAIRS // 2:
                            pe.wait_ge(val_made, 4 * i + 4)
                        pe.wait_ge(pT_made, i * H + h + 1)
                        wait_from(pe, head_made, i * PAIRS + pair)
                        for s in range(2):
                            q = slice(0, T) if s == 0 else slice(P, T)
                            p = slice(0, T) if s == 0 else slice(T, 3 * P)
                            for n in range(2):
                                hh = h - 1 + n
                                mm = nc.tensor.matmul(ps[DQ * n:DQ * n + DQ, HEAD_BANK, q],
                                                      val[:, s, hh * DQ:(hh + 1) * DQ], probT[:, hh % 4, p],
                                                      start=(s == 0), stop=(s == 1), skip_group_check=True)
                        mm.then_inc(head_psum, 1)
                    h = j - 5
                    if h > 0 and h % 2:
                        pair = h // 2
                        pe.wait_ge(head_made, i * PAIRS + pair + 1)
                        if pair == 0:
                            wait_from(pe, res_made, i)
                        for t in range(2):
                            mm = nc.tensor.matmul(ps[:, OUT_BANK, t * E:(t + 1) * E],
                                                  headT[:, pair % 2, t * P:(t + 1) * P], wproj[:, pair, :],
                                                  start=(pair == 0 and t == 0), stop=(pair == PAIRS - 1),
                                                  skip_group_check=True)
                        mm.then_inc(out_psum, 1)

            sequence(0, False)
            with pe.Fori(1, B - 1) as i:
                sequence(i, False)
            sequence(B - 1, True)


_INS = ['L0_attn_X', 'L0_attn_Wq', 'L0_attn_bq', 'L0_attn_Wk', 'L0_attn_Wv', 'L0_attn_Wproj', 'L0_attn_bproj',
        'L0_attn_Wr', 'L0_attn_br', 'L0_attn_b_nd', 'L0_ffn_router_w', 'L0_ffn_w1', 'L0_ffn_b1', 'L0_ffn_w2', 'L0_ffn_b2']
_OUTS = [((32, 256, 128), 'float32')]


def kernel(**inputs):
    import numpy as _np
    import concourse.bacc as _bacc
    from concourse import mybir as _mybir
    from concourse.bass_utils import run_bass_kernel_spmd as _run

    nc = _bacc.Bacc("TRN2", target_bir_lowering=False, num_devices=1)
    arrays, args = {}, []
    for name in _INS:
        a = _np.ascontiguousarray(inputs[name])
        arrays[f"in_{name}_dram"] = a
        args.append(nc.dram_tensor(f"in_{name}_dram", a.shape, _mybir.dt.from_np(a.dtype), kind="ExternalInput").ap())
    for i, (shape, dtype) in enumerate(_OUTS):
        dt = _mybir.dt.from_np(_np.dtype(dtype))
        args.append(nc.dram_tensor(f"out_{i}_dram", shape, dt, kind="ExternalOutput").ap())
    build(nc, *args)
    r = _run(nc, [arrays], core_ids=[0])
    got = tuple(r.results[0][f"out_{i}_dram"] for i in range(len(_OUTS)))
    return got[0]
```

```python
from contextlib import ExitStack

import concourse.bass as bass
from concourse import mybir

ALU = mybir.AluOpType
ACT = mybir.ActivationFunctionType
AX_X = mybir.AxisListType.X
F32 = mybir.dt.float32
F32R = mybir.dt.float32r

P = 128
BANK = 512
NEG = -1.0e9
BIG = 3.0e38
EPS = 1e-5


def at(start, size):
    return slice(start, start + size) if isinstance(start, int) else bass.ds(start, size)


def here(i, h, heads):
    return heads if h >= 0 else not isinstance(i, int) or i > 0


def wait_from(engine, semaphore, value):
    if not isinstance(value, int) or value > 0:
        engine.wait_ge(semaphore, value)


def wait_apart(engine, semaphore, value, met):
    if isinstance(value, int):
        wait_from(engine, semaphore, value)
    else:
        value = engine.to_reg(value)
        engine.wait_ge(met, 1)
        engine.wait_ge(semaphore, value)


def build(nc, X, Wq, bq, Wk, Wv, Wproj, bproj, Wr, br, b_nd, router_w, w1, b1, w2, b2, out):
    B, T, E = X.shape
    NB, WIN = b_nd.shape
    H = Wr.shape[1] // NB
    DQ = Wq.shape[1] // H
    NX, FF, _ = w1.shape
    TILES = B * T // P
    PAIRS = H // 2
    FC = FF // P
    BLOCKS = B * T // BANK
    PER = BANK // P
    GROUPS = H // PER
    SCALE = 1.0 / float(DQ) ** 0.5
    assert E == P and WIN == P and T == 2 * P and 2 * DQ == P and FC == 4 and NX == 8 and H == 16

    ctx = ExitStack()
    with ctx:
        top = [((nc.sbuf_base + 31) // 32) * 32]

        def sb(name, shape, dt=F32):
            size = 4
            for n in shape[1:]:
                size *= n
            t = nc.alloc_sbuf_tensor_at(name, shape, dt, offset=top[0])
            top[0] += (size + 31) // 32 * 32
            return t

        def sem(name):
            return ctx.enter_context(nc.semaphore(name))

        acc = sb("acc", [P, TILES, E])
        xnT = sb("xnT", [P, B * T])
        wm_hi = sb("wm_hi", [P, H, P], F32R)
        wm_lo = sb("wm_lo", [P, H, P], F32R)
        wg_hi = sb("wg_hi", [P, H * P], F32R)
        wg_lo = sb("wg_lo", [P, H * P], F32R)
        wv_hi = sb("wv_hi", [P, H * DQ], F32R)
        wv_lo = sb("wv_lo", [P, H * DQ], F32R)
        wproj = sb("wproj", [P, PAIRS, E])
        qbias = sb("qbias", [P, 2, PAIRS])
        ident = sb("ident", [P, P])
        wgt = sb("wgt", [P, TILES, NX])
        b1T = sb("b1T", [P, NX * FC])
        b2r = sb("b2r", [NX, E])
        brev = sb("brev", [NB, WIN])
        brT = sb("brT", [NB, H])
        shared = top[0]

        w1_hi = sb("w1_hi", [P, NX * FC, P], F32R)
        w1_lo = sb("w1_lo", [P, NX * FC, P], F32R)
        w2T = sb("w2T", [P, NX, FC, E])
        xb_hi = sb("xb_hi", [P, BANK], F32R)
        xb_lo = sb("xb_lo", [P, BANK], F32R)
        wblk = sb("wblk", [P, PER, NX])
        wbT = sb("wbT", [NX, PER, P])
        hid_at = top[0]
        hid = sb("hid", [P, 2, FC, BANK])
        prep_at = top[0]

        top[0] = hid_at
        stage = sb("stage", [P, NX * FC, P])
        top[0] = prep_at
        wv_r = sb("wv_r", [P, H * DQ])
        wrT = sb("wrT", [NB, H, P])
        lg = sb("lg", [P, TILES, NX])
        lg2 = sb("lg2", [P, TILES, NX])
        hit = sb("hit", [P, TILES, NX])
        one1 = sb("one1", [P, TILES, NX])
        m1 = sb("m1", [P, TILES])
        m2 = sb("m2", [P, TILES])
        r1 = sb("r1", [P, TILES])
        ex = sb("ex", [P, TILES])
        den = sb("den", [P, TILES])
        rank = sb("rank", [P, NX])
        bproj_bc = sb("bproj_bc", [P, E])
        rwT = sb("rwT", [P, NX])
        assert top[0] <= nc.sbuf_usable_end, (top[0], nc.sbuf_usable_end)
        top[0] = shared
        wq_r = sb("wq_r", [P, H * DQ])
        wk_r = sb("wk_r", [P, H * DQ])
        wqT = sb("wqT", [P, PAIRS, P])
        wkT = sb("wkT", [P, PAIRS, P])
        xn = sb("xn", [P, 2, PER, P])
        wr_r = sb("wr_r", [P, H * NB])
        stats = sb("stats", [P, TILES, 6])
        mean = sb("mean", [P, TILES])
        var = sb("var", [P, TILES])
        std = sb("std", [P, TILES])
        rstd = sb("rstd", [P, TILES])
        lgT = sb("lgT", [NX, BANK])
        rw_r = sb("rw_r", [NX, E])
        b_r = sb("b_r", [NB, WIN])
        bT = sb("bT", [P, NB])
        b1_r = sb("b1_r", [NX * FC, P])
        bq_r = sb("bq_r", [PAIRS, P])
        bqT = sb("bqT", [P, PAIRS])
        br_r = sb("br_r", [H, NB])
        flip = sb("flip", [P, P])
        assert top[0] <= shared + 2 * NX * FC * P * 4, top[0] - shared

        top[0] = shared
        extra = sb("extra", [P, H, 3 * P])
        val = sb("val", [P, 2, H * DQ])
        gbias = sb("gbias", [P, H * P])
        br_rep = sb("br_rep", [NB, H, P])
        gst = sb("gst", [P, 2, BANK])
        xg_hi = sb("xg_hi", [P, T], F32R)
        xg_lo = sb("xg_lo", [P, T], F32R)
        xq_hi = sb("xq_hi", [P, 2 * T], F32R)
        xq_lo = sb("xq_lo", [P, 2 * T], F32R)
        qry = sb("qry", [P, 2, T])
        logit = sb("logit", [P, 2, 3 * P])
        low = sb("low", [P, 2, 2])
        prob = sb("prob", [P, 4, 3 * P])
        total = sb("total", [P, 4, 2])
        inv = sb("inv", [P, 4, 2])
        probT = sb("probT", [P, 4, 3 * P])
        headT = sb("headT", [P, 2, T])
        res = sb("res", [P, 2, E])
        fill = sb("fill", [P, H * P])
        assert top[0] <= nc.sbuf_usable_end, top[0]

        ps = ctx.enter_context(nc.psum_tensor("ps", [P, 8, BANK], F32))

        ROW = 2 * P
        skew = nc.dram_tensor("skew", [2 * H * P * ROW], F32)

        def skew_rows(tile, head, count, first, size, pitch):
            return bass.AP(skew, (tile * H + head) * P * ROW + first,
                           [[pitch, P], [P * ROW, count], [1, size]])

        x_in = [sem(f"x_in{q}") for q in range(4)]
        small_in = sem("small_in")
        w2_in = sem("w2_in")
        w1_in = sem("w1_in")
        attn_in = sem("attn_in")
        const_made = sem("const_made")
        stats_made = sem("stats_made")
        var_ready = sem("var_ready")
        std_ready = sem("std_ready")
        rstd_ready = sem("rstd_ready")
        route_chain = sem("route_chain")
        prep_made = sem("prep_made")
        prep_high = sem("prep_high")
        prep_low = sem("prep_low")
        wv_split = sem("wv_split")
        xn_made = sem("xn_made")
        xnT_psum = sem("xnT_psum")
        xnT_made = sem("xnT_made")
        lgT_psum = sem("lgT_psum")
        lgT_made = sem("lgT_made")
        lg_psum = sem("lg_psum")
        lg_made = sem("lg_made")
        bproj_added = sem("bproj_added")
        route = sem("route")
        route_exp = sem("route_exp")
        block_x = sem("block_x")
        wbT_psum = sem("wbT_psum")
        wbT_made = sem("wbT_made")
        b2_psum = sem("b2_psum")
        b2_added = sem("b2_added")
        hid_psum = sem("hid_psum")
        hid_made = sem("hid_made")
        y_psum = sem("y_psum")
        y_added = sem("y_added")
        fill_made = sem("fill_made")
        filled = sem("filled")
        rep_made = sem("rep_made")
        gb_psum = sem("gb_psum")
        gb_made = sem("gb_made")
        xg_made = sem("xg_made")
        xq_made = sem("xq_made")
        misc_psum = sem("misc_psum")
        val_made = sem("val_made")
        g_staged = sem("g_staged")
        skew_out = [sem(f"skew_out{n}") for n in range(2)]
        skew_in = [sem(f"skew_in{u}") for u in range(2 * GROUPS)]
        q_psum = sem("q_psum")
        q_made = sem("q_made")
        s_psum = sem("s_psum")
        logit_made = sem("logit_made")
        prob_made = sem("prob_made")
        inv_made = sem("inv_made")
        norm_made = sem("norm_made")
        pT_psum = sem("pT_psum")
        pT_made = sem("pT_made")
        head_psum = sem("head_psum")
        head_made = sem("head_made")
        out_psum = sem("out_psum")
        res_made = sem("res_made")
        out_done = sem("out_done")

        PREP = [("w2", NX, False), ("small", 5, False), ("wq", 2, False), ("wk", 2, False), ("wr", 4, False),
                ("brev", 1, False), ("qbias", 2, False), ("wm", 4, True), ("wg", 4, True), ("w1", NX, True)]
        FIRST, SPLITS_BEFORE = {}, []
        n = s = 0
        for name, count, split in PREP:
            FIRST[name] = n
            for _ in range(count):
                SPLITS_BEFORE.append(s)
                s += split
            n += count
        PREP_GROUPS, PREP_SPLITS = n, s
        RING = 4

        XT_BANK, LGT_BANK, LG_BANK = (4, 5), 6, 7
        H_BANK, Y_BANK, WB_BANK, B2_BANK = (0, 1, 2, 3), (4, 5), 6, 7
        Q_BANK, S_BANK, PT_BANK, HEAD_BANK, MISC_BANK, OUT_BANK = (0, 1), (2, 3), 4, 5, 6, 7

        UNITS = [(0, "v", 0, 1, 0), (1, "g", 3, 0, 0), (2, "g", 3, 1, 0), (4, "v", 1, 0, 0), (5, "v", 1, 1, 0),
                 (8, "g", 0, 0, 1), (9, "g", 0, 1, 1), (10, "g", 1, 0, 1), (11, "g", 1, 1, 1), (12, "g", 2, 0, 1),
                 (13, "g", 2, 1, 1), (15, "v", 0, 0, 1)]
        START = [("g", g, t) for g in range(GROUPS - 1) for t in range(2)] + [("v", 0, 0)]
        LAG = 6
        LAST_OWN = 5
        G_UNITS = 2 * GROUPS

        def wm_heads(w, k):
            a = 8 * (k // 2)
            return w[:, a:a + 8, :].rearrange("p (n two) e -> p two n e", two=2)[:, k % 2, :, :]

        def bank4(g):
            return ps[:, g % RING, :].rearrange("p (n e) -> p n e", n=4)

        block = ctx.enter_context(nc.Block())

        @block.sync
        def _(sp):
            x_v = X.rearrange("b (u p) e -> p (b u) e", p=P)
            sp.dma_start(acc[:, 0:16, :], x_v[:, 0:16, :]).then_inc(x_in[0], 16)
            sp.dma_start(stage[:, :, :].rearrange("p (e c) f -> p e (c f)", e=NX),
                         w2.rearrange("e h f -> h e f")).then_inc(w2_in, 16)
            for q in range(1, 4):
                sp.dma_start(acc[:, 16 * q:16 * q + 16, :], x_v[:, 16 * q:16 * q + 16, :]).then_inc(x_in[q], 16)
            sp.dma_start(rw_r[:, :], router_w).then_inc(small_in, 16)
            sp.dma_start(b_r[:, :], b_nd).then_inc(small_in, 16)
            sp.dma_start(b1_r[:, :], b1.rearrange("e (c f) -> (e c) f", c=FC)).then_inc(small_in, 16)
            sp.dma_start(bq_r[:, :], bq.rearrange("(k d) -> k d", d=P)).then_inc(small_in, 16)
            sp.dma_start(br_r[:, :], br.rearrange("(h n) -> h n", n=NB)).then_inc(small_in, 16)
            sp.dma_start(b2r[:, :], b2).then_inc(small_in, 16)
            sp.dma_start(bproj_bc[:, :], bproj.partition_broadcast(P)).then_inc(small_in, 16)
            sp.dma_start(wq_r[:, :], Wq).then_inc(attn_in, 16)
            sp.dma_start(wk_r[:, :], Wk).then_inc(attn_in, 16)
            sp.dma_start(wr_r[:, :], Wr).then_inc(attn_in, 16)
            sp.dma_start(wv_r[:, :], Wv).then_inc(attn_in, 16)
            sp.dma_start(wproj[:, :, :], Wproj.rearrange("(k d) e -> d k e", d=P)).then_inc(attn_in, 16)
            sp.wait_ge(prep_made, FIRST["small"])
            sp.dma_start(stage[:, :, :], w1.rearrange("e (c f) h -> f (e c) h", c=FC)).then_inc(w1_in, 16)

            sp.wait_ge(fill_made, 1)
            for tile in range(2):
                sp.dma_start(skew_rows(tile, 0, H, P, P, ROW),
                             fill[:, :].rearrange("p (h j) -> p h j", h=H)).then_inc(filled, 16)

            def write_unit(k, g, t):
                wait_apart(sp, g_staged, k + 1, filled)
                sp.dma_start(skew_rows(t, PER * g, PER, 0, P, ROW),
                             gst[:, t, :].rearrange("p (h j) -> p h j", h=PER)
                             ).then_inc(skew_out[t], 16)

            def read_unit(i, g, t):
                wait_apart(sp, skew_out[t], (i * GROUPS + g + 1) * 16, filled)
                wait_apart(sp, logit_made, i * H + PER * (g + 1) - H, filled)
                if t == 0:
                    dst, src = extra[:, PER * g:PER * g + PER, 0:P], skew_rows(0, PER * g, PER, P - 1, P, ROW - 1)
                else:
                    dst, src = extra[:, PER * g:PER * g + PER, P:3 * P], skew_rows(1, PER * g, PER, -1, 2 * P, ROW - 1)
                sp.dma_start(dst, src).then_inc(skew_in[2 * g + t], 16)

            def positions(i, groups):
                last = None
                for g in groups:
                    for t in range(2):
                        wait_apart(sp, skew_in[2 * g + t], i * 16, filled)
                        write_unit(i * G_UNITS + 2 * g + t, g, t)
                        if last:
                            read_unit(i, *last)
                        last = (g, t)
                read_unit(i, *last)

            sp.wait_ge(filled, 32)
            positions(0, range(GROUPS - 1))

            out_v = out.rearrange("b (u p) e -> p (b u) e", p=P)

            def store(i):
                sp.wait_ge(res_made, i + 1)
                sp.dma_start(out_v[:, at(2 * i, 2), :], res[:, :, :]).then_inc(out_done, 16)

            positions(0, [GROUPS - 1])
            positions(1, range(GROUPS - 1))
            with sp.Fori(1, B - 1) as i:
                positions(i, [GROUPS - 1])
                store(i - 1)
                positions(i + 1, range(GROUPS - 1))
            positions(B - 1, [GROUPS - 1])
            store(B - 2)
            store(B - 1)
            sp.wait_ge(out_done, 16 * B)

        @block.gpsimd
        def _(pool):
            nc.gpsimd.memset(ident[:, :], 0.0).then_inc(const_made, 1)
            nc.gpsimd.memset(flip[:, :], 0.0).then_inc(const_made, 1)
            for e in range(NX):
                nc.gpsimd.memset(rank[:, e:e + 1], float(NX - e)).then_inc(const_made, 1)
            pool.wait_ge(const_made, 2 + NX)
            nc.gpsimd.affine_select(out=ident[:, :], in_=ident[:, :], compare_op=ALU.not_equal, fill=1.0, base=0,
                                    pattern=[[-1, P]], channel_multiplier=1).then_inc(const_made, 1)
            nc.gpsimd.affine_select(out=flip[:, :], in_=flip[:, :], compare_op=ALU.not_equal, fill=1.0, base=1 - P,
                                    pattern=[[1, P]], channel_multiplier=1).then_inc(const_made, 1)
            pool.wait_ge(attn_in, 80)
            nc.gpsimd.tensor_scalar(wv_hi[:, :], wv_r[:, :], 1.0, 1.0, ALU.mult, ALU.mult).then_inc(wv_split, 1)
            pool.wait_ge(wv_split, 1)
            nc.gpsimd.tensor_tensor(wv_lo[:, :], wv_r[:, :], wv_hi[:, :].bitcast(F32), ALU.subtract).then_inc(wv_split, 1)
            pool.wait_ge(small_in, 112)
            with pool.Fori(0, BLOCKS) as k:
                wait_apart(pool, xn_made, k + 1, const_made)
                nc.gpsimd.tensor_tensor(acc[:, at(PER * k, PER), :], acc[:, at(PER * k, PER), :],
                                        bproj_bc[:, :].unsqueeze(1).broadcast_to([P, PER, E]),
                                        ALU.add).then_inc(bproj_added, 1)
            pool.wait_ge(y_added, BLOCKS * NX)
            nc.gpsimd.memset(fill[:, :], -NEG).then_inc(fill_made, 1)

            def split(i, hi, lo, made):
                nc.gpsimd.tensor_copy(hi, xnT[:, at(i * T, T)]).then_inc(made, 1)
                wait_apart(pool, made, 2 * i + 1, const_made)
                nc.gpsimd.tensor_tensor(lo, xnT[:, at(i * T, T)], hi.bitcast(F32), ALU.subtract).then_inc(made, 1)

            def split_q(i):
                half = at((i % 2) * T, T)
                split(i, xq_hi[:, half], xq_lo[:, half], xq_made)

            split(0, xg_hi[:, :], xg_lo[:, :], xg_made)
            split_q(0)

            def sequence(i, heads=True, more=True):
                for j in range(H if heads else LAG):
                    h = j - 2
                    if here(i, h, heads):
                        wait_apart(pool, inv_made, i * H + h + 1, const_made)
                        nc.gpsimd.tensor_scalar(prob[:, h % 4, 0:P], prob[:, h % 4, 0:P], inv[:, h % 4, 0:1], 1.0,
                                                ALU.mult, ALU.mult).then_inc(norm_made, 1)
                        nc.gpsimd.tensor_scalar(prob[:, h % 4, P:], prob[:, h % 4, P:], inv[:, h % 4, 1:2], 1.0,
                                                ALU.mult, ALU.mult).then_inc(norm_made, 1)
                    if j == 2 and more:
                        wait_apart(pool, q_psum, i * H, const_made)
                        split_q(i + 1)
                    if j == 6 and more:
                        wait_apart(pool, misc_psum, len(START) + i * len(UNITS) + LAST_OWN, const_made)
                        split(i + 1, xg_hi[:, :], xg_lo[:, :], xg_made)

            sequence(0)
            with pool.Fori(1, B - 1) as i:
                sequence(i)
            sequence(B - 1, more=False)
            sequence(B, heads=False, more=False)

        @block.scalar
        def _(act):
            def prep_copy(g, dst, src, scale=1.0):
                act.wait_ge(prep_made, g + 1)
                nc.scalar.activation(dst, src, ACT.Copy, scale=scale).then_inc(prep_high, 1)

            def bank(g, parts=P, cols=BANK):
                return ps[0:parts, g % RING, 0:cols]

            g = FIRST["w2"]
            for e in range(NX):
                prep_copy(g + e, w2T[:, e, :, :].rearrange("p c h -> p (c h)"), bank(g + e))
            g = FIRST["small"]
            prep_copy(g, rwT[:, :], bank(g, P, NX))
            prep_copy(g + 1, bT[:, :], bank(g + 1, P, NB))
            prep_copy(g + 2, b1T[:, :], bank(g + 2, P, NX * FC))
            prep_copy(g + 3, bqT[:, :], bank(g + 3, P, PAIRS))
            prep_copy(g + 4, brT[:, :], bank(g + 4, NB, H))
            for w, dst in (("wq", wqT), ("wk", wkT)):
                for k in range(2):
                    prep_copy(FIRST[w] + k, dst[:, 4 * k:4 * k + 4, :].rearrange("p k e -> p (k e)"),
                              bank(FIRST[w] + k))
            for k in range(4):
                prep_copy(FIRST["wr"] + k, wrT[:, 4 * k:4 * k + 4, :].rearrange("p k e -> p (k e)"),
                          bank(FIRST["wr"] + k, NB))
            prep_copy(FIRST["brev"], brev[:, :], bank(FIRST["brev"], NB, WIN), -1.0)
            for k in range(2):
                prep_copy(FIRST["qbias"] + k, qbias[:, k, :], bank(FIRST["qbias"] + k, P, PAIRS), -SCALE)
            for k in range(4):
                prep_copy(FIRST["wm"] + k, wm_heads(wm_hi, k), bank4(FIRST["wm"] + k), -SCALE)
            for k in range(4):
                prep_copy(FIRST["wg"] + k, wg_hi[:, k * BANK:(k + 1) * BANK], bank(FIRST["wg"] + k))

            act.wait_ge(var_ready, 1)
            nc.scalar.activation(std[:, :], var[:, :], ACT.Sqrt).then_inc(std_ready, 1)
            for k in range(2):
                act.wait_ge(xnT_psum, k + 1)
                nc.scalar.copy(xnT[:, k * BANK:(k + 1) * BANK], ps[:, XT_BANK[k % 2], :]).then_inc(xnT_made, 1)
            with act.Fori(1, BLOCKS // 2) as kk:
                for u in range(2):
                    act.wait_ge(xnT_psum, 2 * kk + (u + 1))
                    nc.scalar.copy(xnT[:, at((2 * kk + u) * BANK, BANK)],
                                   ps[:, XT_BANK[u], :]).then_inc(xnT_made, 1)
            for e in range(NX):
                prep_copy(FIRST["w1"] + e, w1_hi[:, FC * e:FC * e + FC, :].rearrange("p c f -> p (c f)"),
                          bank(FIRST["w1"] + e))
            act.wait_ge(route, 1)
            nc.scalar.activation(ex[:, :], m2[:, :], ACT.Exp).then_inc(route_exp, 1)

            def experts(i):
                act.wait_ge(wbT_psum, i + 1)
                nc.scalar.copy(wbT[:, :, :].rearrange("e t p -> e (t p)"),
                               ps[0:NX, WB_BANK, :]).then_inc(wbT_made, 1)
                for e in range(NX):
                    for c in range(FC):
                        act.wait_ge(hid_psum, i * (NX * FC) + (FC * e + c + 1))
                        if c == 0:
                            wait_from(act, y_psum, i * NX + e - 1)
                        nc.scalar.activation(hid[:, e % 2, c, :], ps[:, H_BANK[c], :], ACT.Gelu,
                                             bias=b1T[:, FC * e + c:FC * e + c + 1]).then_inc(hid_made, 1)

            experts(0)
            with act.Fori(1, BLOCKS) as i:
                experts(i)

            for k in range(GROUPS):
                act.wait_ge(gb_psum, k + 1)
                nc.scalar.copy(gbias[:, k * BANK:(k + 1) * BANK], ps[:, k % 4, :]).then_inc(gb_made, 1)

            def values(count, half, tile):
                act.wait_ge(misc_psum, count + 1)
                nc.scalar.copy(val[:, tile, half * BANK:(half + 1) * BANK], ps[:, MISC_BANK, :]).then_inc(val_made, 1)

            values(len(START) - 1, 0, 0)

            def sequence(i, heads=True, more=True):
                for j in range(H if heads else LAG):
                    if heads:
                        act.wait_ge(q_psum, i * H + j + 1)
                        wait_from(act, s_psum, i * H + j - 1)
                        nc.scalar.activation(qry[:, j % 2, :], ps[:, Q_BANK[j % 2], 0:T], ACT.Identity,
                                             bias=qbias[:, j % 2, j // 2:j // 2 + 1]).then_inc(q_made, 1)
                    for n, (slot, kind, half, tile, ahead) in enumerate(UNITS):
                        if slot == j and kind == "v" and heads and (more or not ahead):
                            wait_from(act, head_psum, (i + ahead - 1) * PAIRS + (half + 1) * PAIRS // 2)
                            values(len(START) + i * len(UNITS) + n, half, tile)
                    h = j - 1
                    if here(i, h, heads):
                        act.wait_ge(logit_made, i * H + h + 1)
                        wait_from(act, pT_psum, i * H + h - 3)
                        for t, (a, b) in enumerate(((0, P), (P, 3 * P))):
                            nc.scalar.activation(prob[:, h % 4, a:b], logit[:, h % 2, a:b], ACT.Exp, scale=-1.0,
                                                 bias=low[:, h % 2, t:t + 1],
                                                 accum_out=total[:, h % 4, t:t + 1]).then_inc(prob_made, 1)
                    h = j - 4
                    if here(i, h, heads) and h % 2:
                        pair = h // 2
                        act.wait_ge(head_psum, i * PAIRS + (pair + 1))
                        wait_from(act, out_psum, i * PAIRS + (pair - 1))
                        nc.scalar.copy(headT[:, pair % 2, :], ps[:, HEAD_BANK, 0:T]).then_inc(head_made, 1)

            sequence(0)
            with act.Fori(1, B - 1) as i:
                sequence(i)
            sequence(B - 1, more=False)
            sequence(B, heads=False, more=False)

        @block.vector
        def _(dve):
            chain = [0]

            def link(ins):
                chain[0] += 1
                ins.then_inc(route_chain, 1)
                dve.wait_ge(route_chain, chain[0])

            GRP = 8
            for q in range(4):
                dve.wait_ge(x_in[q], 16)
                with dve.Fori(2 * q, 2 * q + 2) as s:
                    for n in range(GRP):
                        ins = nc.vector.bn_stats(stats[:, at(GRP * s + n, 1), :].rearrange("p a b -> p (a b)"),
                                                 acc[:, at(GRP * s + n, 1), :].rearrange("p a b -> p (a b)"))
                    ins.then_inc(stats_made, 1)
            dve.wait_ge(stats_made, TILES // GRP)
            mean_e, dev_e, mean_o, dev_o = (stats[:, :, n] for n in (1, 2, 4, 5))
            link(nc.vector.tensor_tensor(mean[:, :], mean_e, mean_o, ALU.add))
            link(nc.vector.tensor_scalar(mean[:, :], mean[:, :], 0.5, None, ALU.mult))
            link(nc.vector.tensor_tensor(std[:, :], mean_e, mean_o, ALU.subtract))
            link(nc.vector.scalar_tensor_tensor(out=std[:, :], in0=std[:, :], scalar=0.25, in1=std[:, :],
                                                op0=ALU.mult, op1=ALU.mult))
            link(nc.vector.tensor_tensor(var[:, :], dev_e, dev_o, ALU.add))
            link(nc.vector.scalar_tensor_tensor(out=var[:, :], in0=var[:, :], scalar=1.0 / E, in1=std[:, :],
                                                op0=ALU.mult, op1=ALU.add))
            nc.vector.tensor_scalar(var[:, :], var[:, :], EPS, None, ALU.add).then_inc(var_ready, 1)

            def low_part(g, dst, hi, src, scale):
                dve.wait_ge(prep_high, g + 1)
                nc.vector.scalar_tensor_tensor(out=dst, in0=src, scalar=scale, in1=hi, op0=ALU.mult,
                                               op1=ALU.subtract).then_inc(prep_low, 1)

            for k in range(4):
                g = FIRST["wm"] + k
                low_part(g, wm_heads(wm_lo, k), wm_heads(wm_hi, k).bitcast(F32), bank4(g), -SCALE)
            for k in range(4):
                g = FIRST["wg"] + k
                low_part(g, wg_lo[:, k * BANK:(k + 1) * BANK],
                         wg_hi[:, k * BANK:(k + 1) * BANK].bitcast(F32), ps[:, g % RING, :], 1.0)
            dve.wait_ge(std_ready, 1)
            nc.vector.reciprocal(rstd[:, :], std[:, :]).then_inc(rstd_ready, 1)
            dve.wait_ge(rstd_ready, 1)

            def norm_block(k, u):
                wait_from(dve, xnT_psum, k - 1)
                for n in range(PER):
                    ins = nc.vector.tensor_scalar(
                        xn[:, u, n, :], acc[:, at(PER * k + n, 1), :].rearrange("p a b -> p (a b)"),
                        mean[:, at(PER * k + n, 1)], rstd[:, at(PER * k + n, 1)],
                        ALU.subtract, ALU.mult)
                ins.then_inc(xn_made, 1)

            def logits_T(k):
                dve.wait_ge(lgT_psum, k + 1)
                wait_from(dve, lg_psum, k)
                nc.vector.tensor_copy(lgT[:, :], ps[0:NX, LGT_BANK, :]).then_inc(lgT_made, 1)

            def logits(k):
                dve.wait_ge(lg_psum, k + 1)
                nc.vector.tensor_copy(lg[:, at(PER * k, PER), :],
                                      ps[:, LG_BANK, 0:PER * NX].rearrange("p (t e) -> p t e", t=PER)
                                      ).then_inc(lg_made, 1)

            norm_block(0, 0)
            norm_block(1, 1)
            logits_T(0)
            with dve.Fori(1, BLOCKS // 2) as kk:
                for u in range(2):
                    norm_block(2 * kk + u, u)
                    logits(2 * kk + (u - 2))
                    logits_T(2 * kk + (u - 1))
            logits(BLOCKS - 2)
            logits_T(BLOCKS - 1)
            logits(BLOCKS - 1)

            for e in range(NX):
                g = FIRST["w1"] + e
                low_part(g, w1_lo[:, FC * e:FC * e + FC, :].rearrange("p c f -> p (c f)"),
                         w1_hi[:, FC * e:FC * e + FC, :].rearrange("p c f -> p (c f)").bitcast(F32),
                         ps[:, g % RING, :], 1.0)

            wide = [P, TILES, NX]
            ranks = rank[:, :].unsqueeze(1).broadcast_to(wide)

            def over(v):
                return v[:, :].unsqueeze(2).broadcast_to(wide)

            dve.wait_ge(lg_made, BLOCKS)
            dve.wait_ge(const_made, 2 + NX)
            link(nc.vector.tensor_reduce(m1[:, :], lg[:, :, :], AX_X, ALU.max))
            link(nc.vector.tensor_tensor(hit[:, :, :], lg[:, :, :], over(m1), ALU.is_equal))
            link(nc.vector.tensor_tensor(hit[:, :, :], hit[:, :, :], ranks, ALU.mult))
            link(nc.vector.tensor_reduce(r1[:, :], hit[:, :, :], AX_X, ALU.max))
            link(nc.vector.tensor_tensor(one1[:, :, :], hit[:, :, :], over(r1), ALU.is_equal))
            link(nc.vector.scalar_tensor_tensor(out=lg2[:, :, :], in0=one1[:, :, :], scalar=-BIG, in1=lg[:, :, :],
                                                op0=ALU.mult, op1=ALU.add))
            link(nc.vector.tensor_reduce(m2[:, :], lg2[:, :, :], AX_X, ALU.max))
            link(nc.vector.tensor_tensor(hit[:, :, :], lg2[:, :, :], over(m2), ALU.is_equal))
            link(nc.vector.tensor_tensor(hit[:, :, :], hit[:, :, :], ranks, ALU.mult))
            link(nc.vector.tensor_reduce(r1[:, :], hit[:, :, :], AX_X, ALU.max))
            link(nc.vector.tensor_tensor(hit[:, :, :], hit[:, :, :], over(r1), ALU.is_equal))
            nc.vector.tensor_tensor(m2[:, :], m2[:, :], m1[:, :], ALU.subtract).then_inc(route, 1)
            dve.wait_ge(route_exp, 1)
            link(nc.vector.tensor_scalar(den[:, :], ex[:, :], 1.0, None, ALU.add))
            link(nc.vector.reciprocal(m1[:, :], den[:, :]))
            link(nc.vector.tensor_tensor(m2[:, :], ex[:, :], m1[:, :], ALU.mult))
            link(nc.vector.tensor_tensor(one1[:, :, :], one1[:, :, :], over(m1), ALU.mult))
            link(nc.vector.tensor_tensor(hit[:, :, :], hit[:, :, :], over(m2), ALU.mult))
            link(nc.vector.tensor_tensor(wgt[:, :, :], one1[:, :, :], hit[:, :, :], ALU.add))
            dve.wait_ge(bproj_added, BLOCKS)

            def block_in(i):
                wait_from(dve, hid_psum, i * (NX * FC))
                x_blk = xnT[:, at(i * BANK, BANK)]
                nc.vector.tensor_copy(xb_hi[:, :], x_blk).then_inc(block_x, 1)
                nc.vector.tensor_copy(wblk[:, :, :], wgt[:, at(PER * i, PER), :]).then_inc(block_x, 1)
                dve.wait_ge(block_x, 3 * i + 1)
                nc.vector.tensor_tensor(xb_lo[:, :], x_blk, xb_hi[:, :].bitcast(F32), ALU.subtract).then_inc(block_x, 1)

            def experts(i, last):
                dve.wait_ge(b2_psum, i + 1)
                a = acc[:, at(PER * i, PER), :]
                nc.vector.tensor_tensor(a, ps[:, B2_BANK, :].rearrange("p (t e) -> p t e", t=PER), a,
                                        ALU.add).then_inc(b2_added, 1)
                dve.wait_ge(b2_added, i + 1)
                for e in range(NX):
                    if e == NX - 1 and not last:
                        block_in(i + 1)
                    dve.wait_ge(y_psum, i * NX + e + 1)
                    if e:
                        dve.wait_ge(y_added, i * NX + e)
                    for t in range(PER):
                        a = acc[:, at(PER * i + t, 1), :].rearrange("p a b -> p (a b)")
                        ins = nc.vector.scalar_tensor_tensor(out=a, in0=ps[:, Y_BANK[e % 2], t * P:(t + 1) * P],
                                                             scalar=wgt[:, at(PER * i + t, 1), e], in1=a,
                                                             op0=ALU.mult, op1=ALU.add)
                    ins.then_inc(y_added, 1)

            block_in(0)
            experts(0, False)
            with dve.Fori(1, BLOCKS - 1) as i:
                experts(i, False)
            experts(BLOCKS - 1, True)
            dve.wait_ge(y_added, BLOCKS * NX)

            nc.vector.tensor_copy(br_rep[:, :, :], brT[:, :].unsqueeze(2).broadcast_to([NB, H, P])).then_inc(rep_made, 1)

            def positions(count, i, g, t):
                dve.wait_ge(misc_psum, count + 1)
                wait_from(dve, skew_out[t], (i * GROUPS + g) * 16)
                nc.vector.tensor_tensor(gst[:, t, :], ps[:, MISC_BANK, :], gbias[:, g * BANK:(g + 1) * BANK],
                                        ALU.add).then_inc(g_staged, 1)

            dve.wait_ge(gb_made, GROUPS)
            for n, (kind, g, t) in enumerate(START):
                if kind == "g":
                    positions(n, 0, g, t)

            def sequence(i, heads=True, more=True):
                for j in range(H if heads else LAG):
                    for n, (slot, kind, g, t, ahead) in enumerate(UNITS):
                        if slot == j and kind == "g" and heads and (more or not ahead):
                            positions(len(START) + i * len(UNITS) + n, i + ahead, g, t)
                    h = j - 2
                    if here(i, h, heads):
                        dve.wait_ge(prob_made, 2 * (i * H + h + 1))
                        wait_from(dve, norm_made, 2 * (i * H + h - 3))
                        nc.vector.reciprocal(inv[:, h % 4, :], total[:, h % 4, :]).then_inc(inv_made, 1)
                    h = j - 1
                    if here(i, h, heads):
                        wait_apart(dve, s_psum, i * H + h + 1, const_made)
                        wait_apart(dve, prob_made, 2 * (i * H + h - 1), const_made)
                        if h >= 0 and h % PER == 0:
                            wait_apart(dve, skew_in[2 * (h // PER)], (i + 1) * 16, const_made)
                            dve.wait_ge(skew_in[2 * (h // PER) + 1], (i + 1) * 16)
                        for t, (a, b) in enumerate(((0, P), (P, 3 * P))):
                            ins = nc.vector.tensor_tensor_reduce(
                                out=logit[:, h % 2, a:b], in0=ps[:, S_BANK[h % 2], a:b], in1=extra[:, h % H, a:b],
                                scale=1.0, scalar=BIG, op0=ALU.add, op1=ALU.min, accum_out=low[:, h % 2, t:t + 1])
                        ins.then_inc(logit_made, 1)
                    h = j - 3
                    if here(i, h, heads):
                        dve.wait_ge(pT_psum, i * H + h + 1)
                        wait_from(dve, head_psum, i * PAIRS + (h // 2 - 1))
                        nc.vector.tensor_copy(probT[:, h % 4, :], ps[:, PT_BANK, 0:3 * P]).then_inc(pT_made, 1)
                    if j == LAG - 1 and here(i, -1, heads):
                        dve.wait_ge(out_psum, i * PAIRS)
                        wait_from(dve, out_done, (i - 1) * 16)
                        nc.vector.tensor_tensor(res[:, :, :], ps[:, OUT_BANK, 0:2 * E].rearrange("p (t e) -> p t e", t=2),
                                                acc[:, at(2 * (i - 1), 2), :], ALU.add).then_inc(res_made, 1)

            sequence(0)
            with dve.Fori(1, B - 1) as i:
                sequence(i)
            sequence(B - 1, more=False)
            sequence(B, heads=False, more=False)

        @block.tensor
        def _(pe):
            def room(g):
                if g >= RING:
                    pe.wait_ge(prep_high, g - RING + 1)
                    done = SPLITS_BEFORE[g - RING + 1]
                    if done:
                        pe.wait_ge(prep_low, done)
                return g % RING

            pe.wait_ge(const_made, 4 + NX)
            pe.wait_ge(w2_in, 16)
            for e in range(NX):
                b = room(FIRST["w2"] + e)
                for c in range(FC):
                    mm = nc.tensor.transpose(ps[:, b, c * P:(c + 1) * P], stage[:, FC * e + c, :], ident[:, :])
                mm.then_inc(prep_made, 1)
            pe.wait_ge(small_in, 112)
            for k, (src, rows, cols) in enumerate(((rw_r, NX, E), (b_r, NB, WIN), (b1_r, NX * FC, P), (bq_r, PAIRS, P),
                                                   (br_r, H, NB))):
                b = room(FIRST["small"] + k)
                nc.tensor.transpose(ps[0:cols, b, 0:rows], src[:, :], ident[0:rows, 0:rows]).then_inc(prep_made, 1)
            pe.wait_ge(attn_in, 80)
            for w, src in (("wq", wq_r), ("wk", wk_r)):
                for k in range(2):
                    b = room(FIRST[w] + k)
                    for n in range(4):
                        mm = nc.tensor.transpose(ps[:, b, n * P:(n + 1) * P], src[:, (4 * k + n) * P:(4 * k + n + 1) * P],
                                                 ident[:, :])
                    mm.then_inc(prep_made, 1)
            for k in range(4):
                b = room(FIRST["wr"] + k)
                for n in range(4):
                    h = 4 * k + n
                    mm = nc.tensor.transpose(ps[0:NB, b, n * P:(n + 1) * P], wr_r[:, h * NB:(h + 1) * NB], ident[:, :])
                mm.then_inc(prep_made, 1)
            b = room(FIRST["brev"])
            pe.wait_ge(prep_high, FIRST["small"] + 2)
            nc.tensor.matmul(ps[0:NB, b, 0:WIN], bT[:, :], flip[:, :], start=True, stop=True).then_inc(prep_made, 1)
            for k in range(2):
                b = room(FIRST["qbias"] + k)
                pe.wait_ge(prep_high, FIRST["wr"])
                for n in range(PAIRS):
                    rows = slice(DQ * k, DQ * k + DQ)
                    mm = nc.tensor.matmul(ps[:, b, n:n + 1], wkT[rows, n, :], bqT[rows, n:n + 1], start=True, stop=True)
                mm.then_inc(prep_made, 1)

            for k in range(4):
                b = room(FIRST["wm"] + k)
                pe.wait_ge(prep_high, FIRST["wr"])
                for n in range(4):
                    pair = 4 * (k // 2) + n
                    rows = slice(DQ * (k % 2), DQ * (k % 2) + DQ)
                    mm = nc.tensor.matmul(ps[:, b, n * P:(n + 1) * P], wqT[rows, pair, :], wkT[rows, pair, :],
                                          start=True, stop=True)
                mm.then_inc(prep_made, 1)
            for k in range(4):
                b = room(FIRST["wg"] + k)
                pe.wait_ge(prep_high, FIRST["brev"] + 1)
                for n in range(4):
                    mm = nc.tensor.matmul(ps[:, b, n * P:(n + 1) * P], wrT[:, 4 * k + n, :], brev[:, :],
                                          start=True, stop=True)
                mm.then_inc(prep_made, 1)

            def turn(k, u):
                pe.wait_ge(xn_made, k + 1)
                wait_from(pe, xnT_made, k - 1)
                for n in range(PER):
                    mm = nc.tensor.transpose(ps[:, XT_BANK[u], n * P:(n + 1) * P], xn[:, u, n, :], ident[:, :])
                mm.then_inc(xnT_psum, 1)

            def router(k):
                pe.wait_ge(xnT_made, k + 1)
                wait_from(pe, lgT_made, k)
                nc.tensor.matmul(ps[0:NX, LGT_BANK, :], rwT[:, :], xnT[:, at(k * BANK, BANK)],
                                 start=True, stop=True).then_inc(lgT_psum, 1)

            def router_back(k):
                wait_apart(pe, lgT_made, k + 1, const_made)
                wait_apart(pe, lg_made, k, const_made)
                for n in range(PER):
                    mm = nc.tensor.transpose(ps[:, LG_BANK, n * NX:(n + 1) * NX], lgT[:, n * P:(n + 1) * P],
                                             ident[0:NX, 0:NX])
                mm.then_inc(lg_psum, 1)

            pe.wait_ge(prep_high, FIRST["small"] + 1)
            turn(0, 0)
            turn(1, 1)
            router(0)
            with pe.Fori(1, BLOCKS // 2) as kk:
                for u in range(2):
                    router_back(2 * kk + (u - 2))
                    turn(2 * kk + u, u)
                    router(2 * kk + (u - 1))
            router_back(BLOCKS - 2)
            router(BLOCKS - 1)
            router_back(BLOCKS - 1)

            pe.wait_ge(w1_in, 16)
            for e in range(NX):
                b = room(FIRST["w1"] + e)
                for c in range(FC):
                    mm = nc.tensor.transpose(ps[:, b, c * P:(c + 1) * P], stage[:, FC * e + c, :], ident[:, :])
                mm.then_inc(prep_made, 1)
            pe.wait_ge(prep_high, PREP_GROUPS)
            pe.wait_ge(prep_low, PREP_SPLITS)

            def product(dst, parts, start=True, stop=True):
                (a_hi, a_lo), (b_hi, b_lo) = parts
                nc.tensor.matmul(dst, a_hi, b_hi, start=start, stop=False)
                nc.tensor.matmul(dst, a_hi, b_lo, start=False, stop=False)
                return nc.tensor.matmul(dst, a_lo, b_hi, start=False, stop=stop)

            def expert_in(i, e):
                for c in range(FC):
                    wait_from(pe, hid_made, i * (NX * FC) + FC * e + c - FC + 1)
                    product(ps[:, H_BANK[c], :], ((w1_hi[:, FC * e + c, :], w1_lo[:, FC * e + c, :]),
                                                  (xb_hi[:, :], xb_lo[:, :]))).then_inc(hid_psum, 1)

            def expert_out(i, e):
                pe.wait_ge(hid_made, i * (NX * FC) + FC * (e + 1))
                wait_from(pe, y_added, i * NX + e - 1)
                for t in range(PER):
                    for c in range(FC):
                        mm = nc.tensor.matmul(ps[:, Y_BANK[e % 2], t * P:(t + 1) * P],
                                              hid[:, e % 2, c, t * P:(t + 1) * P], w2T[:, e, c, :],
                                              start=(c == 0), stop=(c == FC - 1))
                mm.then_inc(y_psum, 1)

            def experts(i):
                pe.wait_ge(block_x, 3 * i + 3)
                for t in range(PER):
                    mm = nc.tensor.transpose(ps[0:NX, WB_BANK, t * P:(t + 1) * P], wblk[:, t, :], ident[:, :])
                mm.then_inc(wbT_psum, 1)
                expert_in(i, 0)
                pe.wait_ge(wbT_made, i + 1)
                wait_from(pe, b2_added, i)
                for t in range(PER):
                    mm = nc.tensor.matmul(ps[:, B2_BANK, t * P:(t + 1) * P], wbT[:, t, :], b2r[:, :],
                                          start=True, stop=True)
                mm.then_inc(b2_psum, 1)
                for e in range(1, NX):
                    expert_in(i, e)
                    expert_out(i, e - 1)
                expert_out(i, NX - 1)

            experts(0)
            with pe.Fori(1, BLOCKS) as i:
                experts(i)

            pe.wait_ge(rep_made, 1)
            for k in range(GROUPS):
                for n in range(PER):
                    mm = nc.tensor.matmul(ps[:, k % 4, n * P:(n + 1) * P], br_rep[:, PER * k + n, :], brev[:, :],
                                          start=True, stop=True)
                mm.then_inc(gb_psum, 1)
            pe.wait_ge(gb_made, GROUPS)
            pe.wait_ge(wv_split, 2)

            def unit(kind, n, tile, values, positions):
                wait_from(pe, val_made, values)
                wait_from(pe, g_staged, positions)
                w_hi, w_lo = (wg_hi, wg_lo) if kind == "g" else (wv_hi, wv_lo)
                rows, cols = slice(tile * P, (tile + 1) * P), slice(n * BANK, (n + 1) * BANK)
                product(ps[:, MISC_BANK, :], ((xg_hi[:, rows], xg_lo[:, rows]),
                                              (w_hi[:, cols], w_lo[:, cols]))).then_inc(misc_psum, 1)

            pe.wait_ge(xg_made, 2)
            for n, (kind, k, t) in enumerate(START):
                unit(kind, k, t, 0, n)

            def sequence(i, heads=True, more=True):
                n_v, n_g = 1, len(START) - 1
                for j in range(H if heads else LAG):
                    if heads:
                        if j == 0:
                            pe.wait_ge(xq_made, 2 * i + 2)
                        wait_from(pe, q_made, i * H + j - 1)
                        x = at((i % 2) * T, T)
                        product(ps[:, Q_BANK[j % 2], 0:T], ((wm_hi[:, j, :], wm_lo[:, j, :]),
                                                            (xq_hi[:, x], xq_lo[:, x]))).then_inc(q_psum, 1)
                    for n, (slot, kind, k, t, ahead) in enumerate(UNITS):
                        if slot == j and heads and (more or not ahead):
                            if n == LAST_OWN:
                                pe.wait_ge(xg_made, 2 * i + 4)
                            unit(kind, k, t, i * 4 + n_v, i * G_UNITS + n_g)
                            n_v, n_g = n_v + (kind == "v"), n_g + (kind == "g")
                    h = j - 1
                    if here(i, h, heads):
                        pe.wait_ge(q_made, i * H + h + 1)
                        wait_from(pe, logit_made, i * H + h - 1)
                        x0 = i * T if h >= 0 else (i - 1) * T
                        nc.tensor.matmul(ps[:, S_BANK[h % 2], 0:P], qry[:, h % 2, 0:P], xnT[:, at(x0, P)],
                                         start=True, stop=True)
                        nc.tensor.matmul(ps[:, S_BANK[h % 2], P:3 * P], qry[:, h % 2, P:T], xnT[:, at(x0, T)],
                                         start=True, stop=True).then_inc(s_psum, 1)
                    h = j - 3
                    if here(i, h, heads):
                        pe.wait_ge(norm_made, 2 * (i * H + h + 1))
                        wait_from(pe, pT_made, i * H + h)
                        for n in range(3):
                            mm = nc.tensor.transpose(ps[:, PT_BANK, n * P:(n + 1) * P],
                                                     prob[:, h % 4, n * P:(n + 1) * P], ident[:, :])
                        mm.then_inc(pT_psum, 1)
                    h = j - 4
                    if here(i, h, heads) and h % 2:
                        pair = h // 2
                        if pair == 0:
                            pe.wait_ge(val_made, 4 * i + 2)
                        if pair == PAIRS // 2:
                            pe.wait_ge(val_made, 4 * i + 4)
                        pe.wait_ge(pT_made, i * H + h + 1)
                        wait_from(pe, head_made, i * PAIRS + pair)
                        for s in range(2):
                            q = slice(0, T) if s == 0 else slice(P, T)
                            p = slice(0, T) if s == 0 else slice(T, 3 * P)
                            for n in range(2):
                                hh = h - 1 + n
                                v = hh % H * DQ
                                mm = nc.tensor.matmul(ps[DQ * n:DQ * n + DQ, HEAD_BANK, q],
                                                      val[:, s, v:v + DQ], probT[:, hh % 4, p],
                                                      start=(s == 0), stop=(s == 1), skip_group_check=True)
                        mm.then_inc(head_psum, 1)
                    h = j - 5
                    if here(i, h, heads) and h % 2:
                        pair = h // 2
                        pe.wait_ge(head_made, i * PAIRS + (pair + 1))
                        if pair == 0:
                            wait_from(pe, res_made, i)
                        for t in range(2):
                            mm = nc.tensor.matmul(ps[:, OUT_BANK, t * E:(t + 1) * E],
                                                  headT[:, pair % 2, t * P:(t + 1) * P], wproj[:, pair % PAIRS, :],
                                                  start=(pair == 0 and t == 0), stop=(pair == -1),
                                                  skip_group_check=True)
                        mm.then_inc(out_psum, 1)

            sequence(0)
            with pe.Fori(1, B - 1) as i:
                sequence(i)
            sequence(B - 1, more=False)
            sequence(B, heads=False, more=False)


_INS = ['L0_attn_X', 'L0_attn_Wq', 'L0_attn_bq', 'L0_attn_Wk', 'L0_attn_Wv', 'L0_attn_Wproj', 'L0_attn_bproj',
        'L0_attn_Wr', 'L0_attn_br', 'L0_attn_b_nd', 'L0_ffn_router_w', 'L0_ffn_w1', 'L0_ffn_b1', 'L0_ffn_w2', 'L0_ffn_b2']
_OUTS = [((32, 256, 128), 'float32')]


def kernel(**inputs):
    import numpy as _np
    import concourse.bacc as _bacc
    from concourse import mybir as _mybir
    from concourse.bass_utils import run_bass_kernel_spmd as _run

    nc = _bacc.Bacc("TRN2", target_bir_lowering=False, num_devices=1)
    arrays, args = {}, []
    for name in _INS:
        a = _np.ascontiguousarray(inputs[name])
        arrays[f"in_{name}_dram"] = a
        args.append(nc.dram_tensor(f"in_{name}_dram", a.shape, _mybir.dt.from_np(a.dtype), kind="ExternalInput").ap())
    for i, (shape, dtype) in enumerate(_OUTS):
        dt = _mybir.dt.from_np(_np.dtype(dtype))
        args.append(nc.dram_tensor(f"out_{i}_dram", shape, dt, kind="ExternalOutput").ap())
    build(nc, *args)
    r = _run(nc, [arrays], core_ids=[0])
    got = tuple(r.results[0][f"out_{i}_dram"] for i in range(len(_OUTS)))
    return got[0]
```

```python
from contextlib import ExitStack

import concourse.bass as bass
from concourse import mybir

ALU = mybir.AluOpType
ACT = mybir.ActivationFunctionType
AX_X = mybir.AxisListType.X
F32 = mybir.dt.float32
F32R = mybir.dt.float32r
U32 = mybir.dt.uint32
I32 = mybir.dt.int32

P = 128
BANK = 512
NEG = -1.0e9
BIG = 3.0e38
EPS = 1e-5


def at(start, size):
    return slice(start, start + size) if isinstance(start, int) else bass.ds(start, size)


def here(i, h, heads, start):
    return heads if h >= 0 else not isinstance(i, int) or i > start


def wait_from(engine, semaphore, value):
    if not isinstance(value, int) or value > 0:
        engine.wait_ge(semaphore, value)


def wait_apart(engine, semaphore, value, met):
    if isinstance(value, int):
        wait_from(engine, semaphore, value)
    else:
        value = engine.to_reg(value)
        engine.wait_ge(met, 1)
        engine.wait_ge(semaphore, value)


def build(nc, X, Wq, bq, Wk, Wv, Wproj, bproj, Wr, br, b_nd, router_w, w1, b1, w2, b2, out):
    B, T, E = X.shape
    NB, WIN = b_nd.shape
    H = Wr.shape[1] // NB
    DQ = Wq.shape[1] // H
    NX, FF, _ = w1.shape
    TILES = B * T // P
    PAIRS = H // 2
    FC = FF // P
    BLOCKS = B * T // BANK
    PER = BANK // P
    TOP = 2
    PLACES = (TOP * B * T - NX) // BANK + NX
    HALF = B // 2
    GROUPS = H // PER
    SCALE = 1.0 / float(DQ) ** 0.5
    assert E == P and WIN == P and T == 2 * P and 2 * DQ == P and FC == 4 and NX == 8 and H == 16

    ctx = ExitStack()
    with ctx:
        top = [((nc.sbuf_base + 31) // 32) * 32]

        def sb(name, shape, dt=F32):
            size = 4
            for n in shape[1:]:
                size *= n
            t = nc.alloc_sbuf_tensor_at(name, shape, dt, offset=top[0])
            top[0] += (size + 31) // 32 * 32
            return t

        def sem(name):
            return ctx.enter_context(nc.semaphore(name))

        acc = sb("acc", [P, TILES, E])
        xnT = sb("xnT", [P, B * T])
        wm_hi = sb("wm_hi", [P, H, P], F32R)
        wm_lo = sb("wm_lo", [P, H, P], F32R)
        wg_hi = sb("wg_hi", [P, H * P], F32R)
        wg_lo = sb("wg_lo", [P, H * P], F32R)
        wv_hi = sb("wv_hi", [P, H * DQ], F32R)
        wv_lo = sb("wv_lo", [P, H * DQ], F32R)
        wproj = sb("wproj", [P, PAIRS, E])
        qbias = sb("qbias", [P, 2, PAIRS])
        ident = sb("ident", [P, P])
        brev = sb("brev", [NB, WIN])
        brT = sb("brT", [NB, H])
        place = sb("place", [P, TILES, TOP], U32)
        wtop = sb("wtop", [P, TILES, TOP])
        owner = sb("owner", [1, PLACES + 1], U32)
        shared = top[0]

        ROW1, ROW2 = 2 * FF + FC, FF + E
        w1s = sb("w1s", [P, NX, ROW1], F32R)
        w2s = sb("w2s", [P, NX, ROW2])
        stage = sb("stage", [P, NX * FC, P])
        wv_r = sb("wv_r", [P, H * DQ])
        lg = sb("lg", [P, TILES, NX])
        zero = sb("zero", [P, BANK])
        small_at = top[0]
        lg2 = sb("lg2", [P, TILES, NX])
        one2 = sb("one2", [P, TILES, NX])
        one1 = sb("one1", [P, TILES, NX])
        scan = [sb(f"scan{n}", [P, TILES, NX]) for n in range(2)]
        chosen = sb("chosen", [P, TILES, NX])
        m1 = sb("m1", [P, TILES])
        m2 = sb("m2", [P, TILES])
        r1 = sb("r1", [P, TILES])
        ex = sb("ex", [P, TILES])
        den = sb("den", [P, TILES])
        rank = sb("rank", [P, NX])
        tally = sb("tally", [P, NX])
        counts = sb("counts", [P, 2, NX])
        over_by = sb("over_by", [P, NX, BLOCKS])
        ends = [sb(f"ends{n}", [P, NX]) for n in range(2)]
        nblk = sb("nblk", [P, NX])
        first = sb("first", [P, NX])
        past = sb("past", [1, PLACES, NX])
        owner_f = sb("owner_f", [1, PLACES])
        numi = sb("numi", [P, PLACES], I32)
        num = sb("num", [P, PLACES])
        steps = sb("steps", [P, BLOCKS])
        lower = sb("lower", [P, P])
        ones = sb("ones", [P, P])
        bproj_bc = sb("bproj_bc", [P, E])
        b1T = sb("b1T", [P, NX * FC])
        rwT = sb("rwT", [P, NX])
        assert top[0] <= nc.sbuf_usable_end, (top[0], nc.sbuf_usable_end)
        top[0] = small_at
        wq_r = sb("wq_r", [P, H * DQ])
        wk_r = sb("wk_r", [P, H * DQ])
        top[0] = shared
        wqT = sb("wqT", [P, PAIRS, P])
        wkT = sb("wkT", [P, PAIRS, P])
        wrT = sb("wrT", [NB, H, P])
        xn = sb("xn", [P, 2, PER, P])
        wr_r = sb("wr_r", [P, H * NB])
        stats = sb("stats", [P, TILES, 6])
        mean = sb("mean", [P, TILES])
        var = sb("var", [P, TILES])
        std = sb("std", [P, TILES])
        rstd = sb("rstd", [P, TILES])
        lgT = sb("lgT", [NX, BANK])
        rw_r = sb("rw_r", [NX, E])
        b_r = sb("b_r", [NB, WIN])
        bT = sb("bT", [P, NB])
        b1_r = sb("b1_r", [NX * FC, P])
        bq_r = sb("bq_r", [PAIRS, P])
        bqT = sb("bqT", [P, PAIRS])
        br_r = sb("br_r", [H, NB])
        flip = sb("flip", [P, P])
        assert top[0] <= shared + NX * ROW1 * 4, (top[0] - shared, NX * ROW1 * 4)

        top[0] = shared
        w1b = sb("w1b", [P, 2, ROW1], F32R)
        w2b = sb("w2b", [P, 2, ROW2])
        placed = sb("placed", [P, 2, PER, E])
        xb_hi = sb("xb_hi", [P, 2, BANK], F32R)
        xb_lo = sb("xb_lo", [P, 2, BANK], F32R)
        hid = sb("hid", [P, 2, FC, BANK])
        yrow = sb("yrow", [P, 2, PER, E])
        experts_end = top[0]

        top[0] = shared
        extra = sb("extra", [P, H, 3 * P])
        val = sb("val", [P, 2, H * DQ])
        br_rep = sb("br_rep", [NB, H, P])
        gst = sb("gst", [P, 2, BANK])
        xg_hi = sb("xg_hi", [P, T], F32R)
        xg_lo = sb("xg_lo", [P, T], F32R)
        xq_hi = sb("xq_hi", [P, 2 * T], F32R)
        xq_lo = sb("xq_lo", [P, 2 * T], F32R)
        qry = sb("qry", [P, 2, T])
        logit = sb("logit", [P, 2, 3 * P])
        low = sb("low", [P, 2, 2])
        prob = sb("prob", [P, 4, 3 * P])
        total = sb("total", [P, 4, 2])
        inv = sb("inv", [P, 4, 2])
        probT = sb("probT", [P, 4, 3 * P])
        headT = sb("headT", [P, 2, T])
        fill = sb("fill", [P, H * P])
        xrow = sb("xrow", [P, PER, E])
        yget = sb("yget", [P, PER, TOP, E])
        at_now = sb("at_now", [P, PER, TOP], U32)
        gbias = sb("gbias", [P, H * P])
        assert top[0] - H * P * 4 - PER * TOP * 4 - (TOP + 1) * PER * E * 4 >= experts_end
        assert top[0] <= nc.sbuf_usable_end, top[0]

        ps = ctx.enter_context(nc.psum_tensor("ps", [P, 8, BANK], F32))

        ROW = 2 * P
        skew = nc.dram_tensor("skew", [2 * H * P * ROW], F32)
        xn_d = nc.dram_tensor("xn_d", [B * T, E], F32)
        x_place = nc.dram_tensor("x_place", [PLACES * BANK, E], F32)
        y_place = nc.dram_tensor("y_place", [PLACES * BANK, E], F32)
        w1_d = nc.dram_tensor("w1_d", [NX, P, ROW1], F32)
        w2_d = nc.dram_tensor("w2_d", [NX, P, ROW2], F32)

        def skew_rows(tile, head, count, first, size, pitch):
            return bass.AP(skew, (tile * H + head) * P * ROW + first,
                           [[pitch, P], [P * ROW, count], [1, size]])

        x_in = [sem(f"x_in{q}") for q in range(4)]
        small_in = sem("small_in")
        w2_in = sem("w2_in")
        w1_in = sem("w1_in")
        attn_in = sem("attn_in")
        const_made = sem("const_made")
        scan_const = sem("scan_const")
        stats_made = sem("stats_made")
        var_ready = sem("var_ready")
        std_ready = sem("std_ready")
        rstd_ready = sem("rstd_ready")
        route_chain = sem("route_chain")
        prep_made = sem("prep_made")
        prep_high = sem("prep_high")
        prep_low = sem("prep_low")
        wv_split = sem("wv_split")
        xn_made = sem("xn_made")
        xnT_psum = sem("xnT_psum")
        xnT_made = sem("xnT_made")
        lgT_psum = sem("lgT_psum")
        lgT_made = sem("lgT_made")
        lg_psum = sem("lg_psum")
        lg_made = sem("lg_made")
        bproj_added = sem("bproj_added")
        zero_made = sem("zero_made")
        route = sem("route")
        route_exp = sem("route_exp")
        tally_made = sem("tally_made")
        counts_psum = sem("counts_psum")
        w_stored = sem("w_stored")
        b_put = sem("b_put")
        zeroed = sem("zeroed")
        xn_out = [sem(f"xn_out{n}") for n in range(2)]
        xrow_in = sem("xrow_in")
        at_made = sem("at_made")
        spread = sem("spread")
        w1b_in = [sem(f"w1b_in{n}") for n in range(2)]
        w2b_in = [sem(f"w2b_in{n}") for n in range(2)]
        rows_in = [sem(f"rows_in{n}") for n in range(2)]
        xb_psum = sem("xb_psum")
        xb_high = sem("xb_high")
        xb_low = sem("xb_low")
        hid_psum = sem("hid_psum")
        hid_made = sem("hid_made")
        y_psum = sem("y_psum")
        y_made = sem("y_made")
        y_out = [sem(f"y_out{n}") for n in range(2)]
        fetched = sem("fetched")
        added = sem("added")
        fill_made = sem("fill_made")
        filled = sem("filled")
        rep_made = sem("rep_made")
        gb_psum = sem("gb_psum")
        gb_made = sem("gb_made")
        xg_made = sem("xg_made")
        xq_made = sem("xq_made")
        misc_psum = sem("misc_psum")
        val_made = sem("val_made")
        g_staged = sem("g_staged")
        skew_out = [sem(f"skew_out{n}") for n in range(2)]
        skew_in = [sem(f"skew_in{u}") for u in range(2 * GROUPS)]
        q_psum = sem("q_psum")
        q_made = sem("q_made")
        s_psum = sem("s_psum")
        logit_made = sem("logit_made")
        prob_made = sem("prob_made")
        inv_made = sem("inv_made")
        norm_made = sem("norm_made")
        pT_psum = sem("pT_psum")
        pT_made = sem("pT_made")
        head_psum = sem("head_psum")
        head_made = sem("head_made")
        out_psum = sem("out_psum")
        attn_added = sem("attn_added")
        out_done = sem("out_done")

        PREP = [("w2", NX, False), ("small", 5, False), ("wq", 2, False), ("wk", 2, False), ("wr", 4, False),
                ("brev", 1, False), ("qbias", 2, False), ("wm", 4, True), ("wg", 4, True), ("w1", NX, True)]
        FIRST, SPLITS_BEFORE = {}, []
        n = s = 0
        for name, count, split in PREP:
            FIRST[name] = n
            for _ in range(count):
                SPLITS_BEFORE.append(s)
                s += split
            n += count
        PREP_GROUPS, PREP_SPLITS = n, s
        RING = 4

        XT_BANK, LGT_BANK, LG_BANK = (4, 5), 6, 7
        H_BANK, Y_BANK, XB_BANK = (0, 1, 2, 3), (4, 5), (6, 7)
        Q_BANK, S_BANK, PT_BANK, HEAD_BANK, MISC_BANK, OUT_BANK = (0, 1), (2, 3), 4, 5, 6, 7

        UNITS = [(0, "v", 0, 1, 0), (1, "g", 3, 0, 0), (2, "g", 3, 1, 0), (4, "v", 1, 0, 0), (5, "v", 1, 1, 0),
                 (8, "g", 0, 0, 1), (9, "g", 0, 1, 1), (10, "g", 1, 0, 1), (11, "g", 1, 1, 1), (12, "g", 2, 0, 1),
                 (13, "g", 2, 1, 1), (15, "v", 0, 0, 1)]
        START = [("g", g, t) for g in range(GROUPS - 1) for t in range(2)] + [("v", 0, 0)]
        LAG = 6
        LAST_OWN = 5
        G_UNITS = 2 * GROUPS

        def wm_heads(w, k):
            a = 8 * (k // 2)
            return w[:, a:a + 8, :].rearrange("p (n two) e -> p two n e", two=2)[:, k % 2, :, :]

        def bank4(g):
            return ps[:, g % RING, :].rearrange("p (n e) -> p n e", n=4)

        block = ctx.enter_context(nc.Block())

        @block.sync
        def _(sp):
            x_v = X.rearrange("b (u p) e -> p (b u) e", p=P)
            sp.dma_start(acc[:, 0:16, :], x_v[:, 0:16, :]).then_inc(x_in[0], 16)
            sp.dma_start(stage[:, :, :].rearrange("p (e c) f -> p e (c f)", e=NX),
                         w2.rearrange("e h f -> h e f")).then_inc(w2_in, 16)
            for q in range(1, 4):
                sp.dma_start(acc[:, 16 * q:16 * q + 16, :], x_v[:, 16 * q:16 * q + 16, :]).then_inc(x_in[q], 16)
            sp.dma_start(rw_r[:, :], router_w).then_inc(small_in, 16)
            sp.dma_start(b_r[:, :], b_nd).then_inc(small_in, 16)
            sp.dma_start(b1_r[:, :], b1.rearrange("e (c f) -> (e c) f", c=FC)).then_inc(small_in, 16)
            sp.dma_start(bq_r[:, :], bq.rearrange("(k d) -> k d", d=P)).then_inc(small_in, 16)
            sp.dma_start(br_r[:, :], br.rearrange("(h n) -> h n", n=NB)).then_inc(small_in, 16)
            sp.dma_start(bproj_bc[:, :], bproj.partition_broadcast(P)).then_inc(small_in, 16)
            sp.dma_start(w2s[:, :, FF:ROW2], b2.partition_broadcast(P)).then_inc(small_in, 16)
            sp.dma_start(wq_r[:, :], Wq).then_inc(attn_in, 16)
            sp.dma_start(wk_r[:, :], Wk).then_inc(attn_in, 16)
            sp.dma_start(wr_r[:, :], Wr).then_inc(attn_in, 16)
            sp.dma_start(wv_r[:, :], Wv).then_inc(attn_in, 16)
            sp.dma_start(wproj[:, :, :], Wproj.rearrange("(k d) e -> d k e", d=P)).then_inc(attn_in, 16)
            sp.wait_ge(prep_made, FIRST["small"])
            sp.dma_start(stage[:, :, :], w1.rearrange("e (c f) h -> f (e c) h", c=FC)).then_inc(w1_in, 16)

            sp.wait_ge(zero_made, 1)
            zero_v = bass.AP(zero, 0, [[BANK, P], [1, BANK]])
            for n in range(PLACES):
                sp.dma_start(bass.AP(x_place, n * BANK * E, [[BANK, P], [1, BANK]]), zero_v).then_inc(zeroed, 16)

            xn_v = xn_d[:, :].rearrange("(u p) e -> p u e", p=P)

            def keep_rows(k, u):
                wait_apart(sp, xn_made, k + 1, w2_in)
                sp.dma_start(xn_v[:, at(PER * k, PER), :], xn[:, u, :, :]).then_inc(xn_out[u], 16)

            keep_rows(0, 0)
            keep_rows(1, 1)
            with sp.Fori(1, BLOCKS // 2) as kk:
                for u in range(2):
                    keep_rows(2 * kk + u, u)

            sp.wait_ge(prep_high, PREP_GROUPS)
            sp.wait_ge(prep_low, PREP_SPLITS)
            sp.wait_ge(b_put, 1)
            sp.dma_start(w1_d[:, :, :].rearrange("e p c -> p e c"), w1s[:, :, :].bitcast(F32)).then_inc(w_stored, 16)
            sp.dma_start(w2_d[:, :, :].rearrange("e p c -> p e c"), w2s[:, :, :]).then_inc(w_stored, 16)

            sp.wait_ge(fill_made, 1)
            for tile in range(2):
                sp.dma_start(skew_rows(tile, 0, H, P, P, ROW),
                             fill[:, :].rearrange("p (h j) -> p h j", h=H)).then_inc(filled, 16)

            def write_unit(k, g, t):
                wait_apart(sp, g_staged, k + 1, filled)
                sp.dma_start(skew_rows(t, PER * g, PER, 0, P, ROW),
                             gst[:, t, :].rearrange("p (h j) -> p h j", h=PER)
                             ).then_inc(skew_out[t], 16)

            def read_unit(i, g, t):
                wait_apart(sp, skew_out[t], (i * GROUPS + g + 1) * 16, filled)
                wait_apart(sp, logit_made, i * H + PER * (g + 1) - H, filled)
                if t == 0:
                    dst, src = extra[:, PER * g:PER * g + PER, 0:P], skew_rows(0, PER * g, PER, P - 1, P, ROW - 1)
                else:
                    dst, src = extra[:, PER * g:PER * g + PER, P:3 * P], skew_rows(1, PER * g, PER, -1, 2 * P, ROW - 1)
                sp.dma_start(dst, src).then_inc(skew_in[2 * g + t], 16)

            def positions(i, groups):
                last = None
                for g in groups:
                    for t in range(2):
                        wait_apart(sp, skew_in[2 * g + t], i * 16, filled)
                        write_unit(i * G_UNITS + 2 * g + t, g, t)
                        if last:
                            read_unit(i, *last)
                        last = (g, t)
                read_unit(i, *last)

            def fetch_rows(i):
                wait_apart(sp, spread, i * (PER * TOP * 16), filled)
                sp.dma_start(xrow[:, :, :], xn_v[:, at(PER * i, PER), :]).then_inc(xrow_in, 16)

            def spread_body(i):
                positions(i, [GROUPS - 1])
                fetch_rows(i)
                positions(i + 1, range(GROUPS - 1))

            sp.wait_ge(filled, 32)
            for u in range(2):
                sp.wait_ge(xn_out[u], BLOCKS // 2 * 16)
            positions(0, range(GROUPS - 1))
            spread_body(0)
            with sp.Fori(1, HALF - 1) as i:
                spread_body(i)
            positions(HALF - 1, [GROUPS - 1])
            fetch_rows(HALF - 1)

            def first_weights(b, u, k):
                wait_apart(sp, hid_made, (b - 1) * FC, filled)
                e = sp.value_load(owner[0:1, at(b, 1)], min_val=0, max_val=NX - 1)
                sp.dma_start(w1b[:, u, :].bitcast(F32), w1_d[bass.ds(e, 1), :, :].rearrange("a p c -> p (a c)")
                             ).then_inc(w1b_in[u], 16)

            def second_weights(b, u, k):
                wait_apart(sp, y_made, b - 1, filled)
                e = sp.value_load(owner[0:1, at(b, 1)], min_val=0, max_val=NX - 1)
                sp.dma_start(w2b[:, u, :], w2_d[bass.ds(e, 1), :, :].rearrange("a p c -> p (a c)")
                             ).then_inc(w2b_in[u], 16)

            xp_v = x_place[:, :].rearrange("(u p) e -> p u e", p=P)
            yp_v = y_place[:, :].rearrange("(u p) e -> p u e", p=P)

            def block_rows(b, u, k):
                wait_apart(sp, xb_psum, b - 1, filled)
                sp.dma_start(placed[:, u, :, :], xp_v[:, at(PER * b, PER), :]).then_inc(rows_in[u], 16)

            def block_out(b, u, k):
                wait_apart(sp, y_made, b + 1, filled)
                sp.dma_start(yp_v[:, at(PER * b, PER), :], yrow[:, u, :, :]).then_inc(y_out[u], 16)

            def experts(b, u, k):
                second_weights(b, u, k)
                if not isinstance(b, int) or b + 1 < PLACES:
                    first_weights(b + 1, 1 - u, None)
                if not isinstance(b, int) or b + 2 < PLACES:
                    block_rows(b + 2, u, None)
                if not isinstance(b, int) or b > 0:
                    block_out(b - 1, 1 - u, None)

            sp.wait_ge(attn_added, HALF)
            sp.wait_ge(spread, TILES * TOP * 16)
            first_weights(0, 0, 0)
            block_rows(0, 0, 0)
            block_rows(1, 1, 0)
            for b in range(3):
                experts(b, b % 2, b // 2)
            with sp.Fori(2, PLACES // 2) as m:
                experts(2 * m - 1, 1, m - 1)
                experts(2 * m, 0, m)
            for b in range(PLACES - 2, PLACES):
                experts(b, b % 2, b // 2)
            block_out(PLACES - 1, (PLACES - 1) % 2, None)

            out_v = out.rearrange("b (u p) e -> p (b u) e", p=P)

            def store(n):
                sp.wait_ge(added, TOP * (n + 1))
                wait_apart(sp, attn_added, n + HALF + 1, filled)
                sp.dma_start(out_v[:, at(PER * n, PER), :], acc[:, at(PER * n, PER), :]).then_inc(out_done, 16)

            positions(HALF, range(GROUPS - 1))
            positions(HALF, [GROUPS - 1])
            positions(HALF + 1, range(GROUPS - 1))
            with sp.Fori(HALF + 1, B - 1) as i:
                positions(i, [GROUPS - 1])
                store(i - HALF - 1)
                positions(i + 1, range(GROUPS - 1))
            positions(B - 1, [GROUPS - 1])
            store(HALF - 2)
            store(HALF - 1)
            sp.wait_ge(out_done, 16 * HALF)

        @block.gpsimd
        def _(pool):
            nc.gpsimd.memset(ident[:, :], 0.0).then_inc(const_made, 1)
            nc.gpsimd.memset(flip[:, :], 0.0).then_inc(const_made, 1)
            nc.gpsimd.memset(zero[:, :], 0.0).then_inc(zero_made, 1)
            pool.wait_ge(const_made, 2)
            nc.gpsimd.affine_select(out=ident[:, :], in_=ident[:, :], compare_op=ALU.not_equal, fill=1.0, base=0,
                                    pattern=[[-1, P]], channel_multiplier=1).then_inc(const_made, 1)
            nc.gpsimd.affine_select(out=flip[:, :], in_=flip[:, :], compare_op=ALU.not_equal, fill=1.0, base=1 - P,
                                    pattern=[[1, P]], channel_multiplier=1).then_inc(const_made, 1)
            pool.wait_ge(attn_in, 80)
            nc.gpsimd.tensor_scalar(wv_hi[:, :], wv_r[:, :], 1.0, 1.0, ALU.mult, ALU.mult).then_inc(wv_split, 1)
            pool.wait_ge(wv_split, 1)
            nc.gpsimd.tensor_tensor(wv_lo[:, :], wv_r[:, :], wv_hi[:, :].bitcast(F32), ALU.subtract).then_inc(wv_split, 1)
            pool.wait_ge(small_in, 112)
            with pool.Fori(0, BLOCKS) as k:
                wait_apart(pool, xn_made, k + 1, const_made)
                nc.gpsimd.tensor_tensor(acc[:, at(PER * k, PER), :], acc[:, at(PER * k, PER), :],
                                        bproj_bc[:, :].unsqueeze(1).broadcast_to([P, PER, E]),
                                        ALU.add).then_inc(bproj_added, 1)
            pool.wait_ge(prep_made, FIRST["wr"])
            nc.gpsimd.memset(ones[:, :], 1.0).then_inc(scan_const, 1)
            for e in range(NX):
                nc.gpsimd.memset(rank[:, e:e + 1], float(NX - e)).then_inc(scan_const, 1)
            nc.gpsimd.iota(numi[:, :], [[1, PLACES]], base=0, channel_multiplier=0).then_inc(scan_const, 1)
            pool.wait_ge(scan_const, 2 + NX)
            nc.gpsimd.affine_select(out=lower[:, :], in_=ones[:, :], compare_op=ALU.is_gt, fill=0.0, base=0,
                                    pattern=[[1, P]], channel_multiplier=-1).then_inc(scan_const, 1)
            pool.wait_ge(w_stored, 32)
            pool.wait_ge(zeroed, PLACES * 16)
            pool.wait_ge(route, 2)
            nc.gpsimd.memset(fill[:, :], -NEG).then_inc(fill_made, 1)

            def split(i, hi, lo, made):
                nc.gpsimd.tensor_copy(hi, xnT[:, at(i * T, T)]).then_inc(made, 1)
                wait_apart(pool, made, 2 * i + 1, const_made)
                nc.gpsimd.tensor_tensor(lo, xnT[:, at(i * T, T)], hi.bitcast(F32), ALU.subtract).then_inc(made, 1)

            def split_q(i):
                half = at((i % 2) * T, T)
                split(i, xq_hi[:, half], xq_lo[:, half], xq_made)

            table_x = x_place[:, :]
            table_y = y_place[:, :]

            def move_row(i, n):
                t, k = n // TOP, n % TOP
                index = bass.IndirectOffsetOnAxis(at_now[:, t, k:k + 1], 0)
                if i is FORTH:
                    nc.gpsimd.indirect_dma_start(table_x, index, xrow[:, t, :], None).then_inc(spread, 16)
                else:
                    nc.gpsimd.indirect_dma_start(yget[:, t, k, :], None, table_y, index).then_inc(fetched, 16)

            def sequence(i, way, start, heads=True, more=True):
                for j in range(H if heads else LAG):
                    h = j - 2
                    if here(i, h, heads, start):
                        wait_apart(pool, inv_made, i * H + h + 1, const_made)
                        nc.gpsimd.tensor_scalar(prob[:, h % 4, 0:P], prob[:, h % 4, 0:P], inv[:, h % 4, 0:1], 1.0,
                                                ALU.mult, ALU.mult).then_inc(norm_made, 1)
                        nc.gpsimd.tensor_scalar(prob[:, h % 4, P:], prob[:, h % 4, P:], inv[:, h % 4, 1:2], 1.0,
                                                ALU.mult, ALU.mult).then_inc(norm_made, 1)
                    if j == 2 and more:
                        wait_apart(pool, s_psum, i * H, const_made)
                        split_q(i + 1)
                    if j == 6 and more:
                        wait_apart(pool, misc_psum, len(START) + i * len(UNITS) + LAST_OWN, const_made)
                        split(i + 1, xg_hi[:, :], xg_lo[:, :], xg_made)
                    if j == 8 and heads:
                        if way is FORTH:
                            wait_apart(pool, spread, i * (PER * TOP * 16), const_made)
                            first_tile = i * PER
                        else:
                            wait_apart(pool, added, TOP * (i - HALF), const_made)
                            first_tile = (i - HALF) * PER
                        nc.gpsimd.tensor_copy(at_now[:, :, :], place[:, at(first_tile, PER), :]).then_inc(at_made, 1)
                        if way is FORTH:
                            wait_apart(pool, xrow_in, (i + 1) * 16, const_made)
                        wait_apart(pool, at_made, i + 1, const_made)
                    if j >= 8 and heads:
                        move_row(way, j - 8)

            FORTH, BACK = "forth", "back"
            for s0, way in ((0, FORTH), (HALF, BACK)):
                s1 = s0 + HALF
                if way is BACK:
                    pool.wait_ge(y_out[0], (PLACES + 1) // 2 * 16)
                    pool.wait_ge(y_out[1], PLACES // 2 * 16)
                split(s0, xg_hi[:, :], xg_lo[:, :], xg_made)
                split_q(s0)
                sequence(s0, way, s0)
                with pool.Fori(s0 + 1, s1 - 1) as i:
                    sequence(i, way, s0)
                sequence(s1 - 1, way, s0, more=False)
                sequence(s1, way, s0, heads=False, more=False)

        @block.scalar
        def _(act):
            def prep_copy(g, dst, src, scale=1.0):
                act.wait_ge(prep_made, g + 1)
                nc.scalar.activation(dst, src, ACT.Copy, scale=scale).then_inc(prep_high, 1)

            def bank(g, parts=P, cols=BANK):
                return ps[0:parts, g % RING, 0:cols]

            g = FIRST["w2"]
            for e in range(NX):
                prep_copy(g + e, w2s[:, e, 0:FF], bank(g + e))
            g = FIRST["small"]
            prep_copy(g, rwT[:, :], bank(g, P, NX))
            prep_copy(g + 1, bT[:, :], bank(g + 1, P, NB))
            prep_copy(g + 2, b1T[:, :], bank(g + 2, P, NX * FC))
            prep_copy(g + 3, bqT[:, :], bank(g + 3, P, PAIRS))
            prep_copy(g + 4, brT[:, :], bank(g + 4, NB, H))
            for w, dst in (("wq", wqT), ("wk", wkT)):
                for k in range(2):
                    prep_copy(FIRST[w] + k, dst[:, 4 * k:4 * k + 4, :].rearrange("p k e -> p (k e)"),
                              bank(FIRST[w] + k))
            for k in range(4):
                prep_copy(FIRST["wr"] + k, wrT[:, 4 * k:4 * k + 4, :].rearrange("p k e -> p (k e)"),
                          bank(FIRST["wr"] + k, NB))
            prep_copy(FIRST["brev"], brev[:, :], bank(FIRST["brev"], NB, WIN), -1.0)
            for k in range(2):
                prep_copy(FIRST["qbias"] + k, qbias[:, k, :], bank(FIRST["qbias"] + k, P, PAIRS), -SCALE)
            for k in range(4):
                prep_copy(FIRST["wm"] + k, wm_heads(wm_hi, k), bank4(FIRST["wm"] + k), -SCALE)
            for k in range(4):
                prep_copy(FIRST["wg"] + k, wg_hi[:, k * BANK:(k + 1) * BANK], bank(FIRST["wg"] + k))

            act.wait_ge(var_ready, 1)
            nc.scalar.activation(std[:, :], var[:, :], ACT.Sqrt).then_inc(std_ready, 1)
            for k in range(2):
                act.wait_ge(xnT_psum, k + 1)
                nc.scalar.copy(xnT[:, k * BANK:(k + 1) * BANK], ps[:, XT_BANK[k % 2], :]).then_inc(xnT_made, 1)
            with act.Fori(1, BLOCKS // 2) as kk:
                for u in range(2):
                    act.wait_ge(xnT_psum, 2 * kk + (u + 1))
                    nc.scalar.copy(xnT[:, at((2 * kk + u) * BANK, BANK)],
                                   ps[:, XT_BANK[u], :]).then_inc(xnT_made, 1)
            for u in range(2):
                act.wait_ge(xn_out[u], BLOCKS // 2 * 16)
            for e in range(NX):
                prep_copy(FIRST["w1"] + e, w1s[:, e, 0:FF], bank(FIRST["w1"] + e))
            act.wait_ge(route, 1)
            nc.scalar.activation(ex[:, :], m2[:, :], ACT.Exp).then_inc(route_exp, 1)

            for k in range(GROUPS):
                act.wait_ge(gb_psum, k + 1)
                nc.scalar.copy(gbias[:, k * BANK:(k + 1) * BANK], ps[:, k % 4, :]).then_inc(gb_made, 1)

            def values(count, half, tile):
                act.wait_ge(misc_psum, count + 1)
                nc.scalar.copy(val[:, tile, half * BANK:(half + 1) * BANK], ps[:, MISC_BANK, :]).then_inc(val_made, 1)

            def sequence(i, start, heads=True, more=True):
                for j in range(H if heads else LAG):
                    if heads:
                        act.wait_ge(q_psum, i * H + j + 1)
                        wait_from(act, s_psum, i * H + j - 1)
                        nc.scalar.activation(qry[:, j % 2, :], ps[:, Q_BANK[j % 2], 0:T], ACT.Identity,
                                             bias=qbias[:, j % 2, j // 2:j // 2 + 1]).then_inc(q_made, 1)
                    for n, (slot, kind, half, tile, ahead) in enumerate(UNITS):
                        if slot == j and kind == "v" and heads and (more or not ahead):
                            wait_from(act, head_psum, (i + ahead - 1) * PAIRS + (half + 1) * PAIRS // 2)
                            values(len(START) + i * len(UNITS) + n, half, tile)
                    h = j - 1
                    if here(i, h, heads, start):
                        act.wait_ge(logit_made, i * H + h + 1)
                        wait_from(act, pT_psum, i * H + h - 3)
                        for t, (a, b) in enumerate(((0, P), (P, 3 * P))):
                            nc.scalar.activation(prob[:, h % 4, a:b], logit[:, h % 2, a:b], ACT.Exp, scale=-1.0,
                                                 bias=low[:, h % 2, t:t + 1],
                                                 accum_out=total[:, h % 4, t:t + 1]).then_inc(prob_made, 1)
                    h = j - 4
                    if here(i, h, heads, start) and h % 2:
                        pair = h // 2
                        act.wait_ge(head_psum, i * PAIRS + (pair + 1))
                        wait_from(act, out_psum, i * PAIRS + (pair - 1))
                        nc.scalar.copy(headT[:, pair % 2, :], ps[:, HEAD_BANK, 0:T]).then_inc(head_made, 1)

            def experts(b, u, k):
                if not isinstance(b, int) or b + 1 < PLACES:
                    high_part(b + 1, 1 - u)
                for c in range(FC):
                    if c == 0:
                        wait_from(act, y_psum, b - 1)
                        act.wait_ge(w1b_in[u], 16 * k + 16)
                    act.wait_ge(hid_psum, b * FC + c + 1)
                    nc.scalar.activation(hid[:, u, c, :], ps[:, H_BANK[c], :], ACT.Gelu,
                                         bias=w1b[:, u, 2 * FF + c:2 * FF + c + 1].bitcast(F32)).then_inc(hid_made, 1)

            def high_part(b, u):
                act.wait_ge(xb_psum, b + 1)
                wait_from(act, hid_psum, (b - 1) * FC)
                nc.scalar.copy(xb_hi[:, u, :], ps[:, XB_BANK[u], :]).then_inc(xb_high, 1)

            for s0 in (0, HALF):
                s1 = s0 + HALF
                values(len(START) - 1 + s0 * len(UNITS), 0, 0)
                sequence(s0, s0)
                with act.Fori(s0 + 1, s1 - 1) as i:
                    sequence(i, s0)
                sequence(s1 - 1, s0, more=False)
                sequence(s1, s0, heads=False, more=False)
                if s0 == 0:
                    high_part(0, 0)
                    for b in range(3):
                        experts(b, b % 2, b // 2)
                    with act.Fori(2, PLACES // 2) as m:
                        experts(2 * m - 1, 1, m - 1)
                        experts(2 * m, 0, m)
                    for b in range(PLACES - 2, PLACES):
                        experts(b, b % 2, b // 2)

        @block.vector
        def _(dve):
            chain = [0]

            def link(ins):
                chain[0] += 1
                ins.then_inc(route_chain, 1)
                dve.wait_ge(route_chain, chain[0])

            GRP = 8
            for q in range(4):
                dve.wait_ge(x_in[q], 16)
                with dve.Fori(2 * q, 2 * q + 2) as s:
                    for n in range(GRP):
                        ins = nc.vector.bn_stats(stats[:, at(GRP * s + n, 1), :].rearrange("p a b -> p (a b)"),
                                                 acc[:, at(GRP * s + n, 1), :].rearrange("p a b -> p (a b)"))
                    ins.then_inc(stats_made, 1)
            dve.wait_ge(stats_made, TILES // GRP)
            mean_e, dev_e, mean_o, dev_o = (stats[:, :, n] for n in (1, 2, 4, 5))
            link(nc.vector.tensor_tensor(mean[:, :], mean_e, mean_o, ALU.add))
            link(nc.vector.tensor_scalar(mean[:, :], mean[:, :], 0.5, None, ALU.mult))
            link(nc.vector.tensor_tensor(std[:, :], mean_e, mean_o, ALU.subtract))
            link(nc.vector.scalar_tensor_tensor(out=std[:, :], in0=std[:, :], scalar=0.25, in1=std[:, :],
                                                op0=ALU.mult, op1=ALU.mult))
            link(nc.vector.tensor_tensor(var[:, :], dev_e, dev_o, ALU.add))
            link(nc.vector.scalar_tensor_tensor(out=var[:, :], in0=var[:, :], scalar=1.0 / E, in1=std[:, :],
                                                op0=ALU.mult, op1=ALU.add))
            nc.vector.tensor_scalar(var[:, :], var[:, :], EPS, None, ALU.add).then_inc(var_ready, 1)

            def low_part(g, dst, hi, src, scale):
                dve.wait_ge(prep_high, g + 1)
                nc.vector.scalar_tensor_tensor(out=dst, in0=src, scalar=scale, in1=hi, op0=ALU.mult,
                                               op1=ALU.subtract).then_inc(prep_low, 1)

            for k in range(4):
                g = FIRST["wm"] + k
                low_part(g, wm_heads(wm_lo, k), wm_heads(wm_hi, k).bitcast(F32), bank4(g), -SCALE)
            for k in range(4):
                g = FIRST["wg"] + k
                low_part(g, wg_lo[:, k * BANK:(k + 1) * BANK],
                         wg_hi[:, k * BANK:(k + 1) * BANK].bitcast(F32), ps[:, g % RING, :], 1.0)
            dve.wait_ge(std_ready, 1)
            nc.vector.reciprocal(rstd[:, :], std[:, :]).then_inc(rstd_ready, 1)
            dve.wait_ge(rstd_ready, 1)

            def norm_block(k, u, half):
                wait_from(dve, xnT_psum, k - 1)
                wait_from(dve, xn_out[u], half * 16)
                for n in range(PER):
                    ins = nc.vector.tensor_scalar(
                        xn[:, u, n, :], acc[:, at(PER * k + n, 1), :].rearrange("p a b -> p (a b)"),
                        mean[:, at(PER * k + n, 1)], rstd[:, at(PER * k + n, 1)],
                        ALU.subtract, ALU.mult)
                ins.then_inc(xn_made, 1)

            def logits_T(k):
                dve.wait_ge(lgT_psum, k + 1)
                wait_from(dve, lg_psum, k)
                nc.vector.tensor_copy(lgT[:, :], ps[0:NX, LGT_BANK, :]).then_inc(lgT_made, 1)

            def logits(k):
                dve.wait_ge(lg_psum, k + 1)
                nc.vector.tensor_copy(lg[:, at(PER * k, PER), :],
                                      ps[:, LG_BANK, 0:PER * NX].rearrange("p (t e) -> p t e", t=PER)
                                      ).then_inc(lg_made, 1)

            norm_block(0, 0, 0)
            norm_block(1, 1, 0)
            logits_T(0)
            with dve.Fori(1, BLOCKS // 2) as kk:
                for u in range(2):
                    norm_block(2 * kk + u, u, kk)
                    logits(2 * kk + (u - 2))
                    logits_T(2 * kk + (u - 1))
            logits(BLOCKS - 2)
            logits_T(BLOCKS - 1)
            logits(BLOCKS - 1)

            for u in range(2):
                dve.wait_ge(xn_out[u], BLOCKS // 2 * 16)
            for e in range(NX):
                g = FIRST["w1"] + e
                low_part(g, w1s[:, e, FF:2 * FF], w1s[:, e, 0:FF].bitcast(F32), ps[:, g % RING, :], 1.0)
            nc.vector.tensor_copy(w1s[:, :, 2 * FF:ROW1], b1T[:, :].rearrange("p (e c) -> p e c", c=FC)
                                  ).then_inc(b_put, 1)

            wide = [P, TILES, NX]
            ranks = rank[:, :].unsqueeze(1).broadcast_to(wide)

            def over(v):
                return v[:, :].unsqueeze(2).broadcast_to(wide)

            dve.wait_ge(lg_made, BLOCKS)
            dve.wait_ge(scan_const, 3 + NX)
            link(nc.vector.tensor_reduce(m1[:, :], lg[:, :, :], AX_X, ALU.max))
            link(nc.vector.tensor_tensor(one2[:, :, :], lg[:, :, :], over(m1), ALU.is_equal))
            link(nc.vector.tensor_tensor(one2[:, :, :], one2[:, :, :], ranks, ALU.mult))
            link(nc.vector.tensor_reduce(r1[:, :], one2[:, :, :], AX_X, ALU.max))
            link(nc.vector.tensor_tensor(one1[:, :, :], one2[:, :, :], over(r1), ALU.is_equal))
            link(nc.vector.scalar_tensor_tensor(out=lg2[:, :, :], in0=one1[:, :, :], scalar=-BIG, in1=lg[:, :, :],
                                                op0=ALU.mult, op1=ALU.add))
            link(nc.vector.tensor_reduce(m2[:, :], lg2[:, :, :], AX_X, ALU.max))
            link(nc.vector.tensor_tensor(one2[:, :, :], lg2[:, :, :], over(m2), ALU.is_equal))
            link(nc.vector.tensor_tensor(one2[:, :, :], one2[:, :, :], ranks, ALU.mult))
            link(nc.vector.tensor_reduce(r1[:, :], one2[:, :, :], AX_X, ALU.max))
            link(nc.vector.tensor_tensor(one2[:, :, :], one2[:, :, :], over(r1), ALU.is_equal))
            nc.vector.tensor_tensor(m2[:, :], m2[:, :], m1[:, :], ALU.subtract).then_inc(route, 1)
            link(nc.vector.tensor_tensor(chosen[:, :, :], one1[:, :, :], one2[:, :, :], ALU.add))
            src, d = chosen, 1
            while d < TILES:
                dst = scan[0] if src is not scan[0] else scan[1]
                nc.vector.tensor_copy(dst[:, 0:d, :], src[:, 0:d, :])
                link(nc.vector.tensor_tensor(dst[:, d:, :], src[:, d:, :], src[:, 0:TILES - d, :], ALU.add))
                src, d = dst, 2 * d
            upto = src
            nc.vector.tensor_copy(tally[:, :], upto[:, TILES - 1, :]).then_inc(tally_made, 1)
            dve.wait_ge(counts_psum, 1)
            link(nc.vector.tensor_copy(counts[:, :, :], ps[:, 0, 0:2 * NX].rearrange("p (a e) -> p a e", a=2)))
            link(nc.vector.tensor_copy(num[:, :], numi[:, :]))
            link(nc.vector.tensor_scalar(steps[:, :], num[:, 0:BLOCKS], float(BANK), None, ALU.mult))
            per_step = [P, NX, BLOCKS]
            link(nc.vector.tensor_tensor(over_by[:, :, :], counts[:, 1, :].unsqueeze(2).broadcast_to(per_step),
                                         steps[:, :].unsqueeze(1).broadcast_to(per_step), ALU.is_gt))
            link(nc.vector.tensor_reduce(nblk[:, :], over_by[:, :, :], AX_X, ALU.add))
            src, d = nblk, 1
            while d < NX:
                dst = ends[0] if src is not ends[0] else ends[1]
                nc.vector.tensor_copy(dst[:, 0:d], src[:, 0:d])
                link(nc.vector.tensor_tensor(dst[:, d:], src[:, d:], src[:, 0:NX - d], ALU.add))
                src, d = dst, 2 * d
            end = src
            per_block = [1, PLACES, NX]
            link(nc.vector.tensor_tensor(past[:, :, :], num[0:1, :].unsqueeze(2).broadcast_to(per_block),
                                         end[0:1, :].unsqueeze(1).broadcast_to(per_block), ALU.is_ge))
            link(nc.vector.tensor_reduce(owner_f[:, :], past[:, :, :], AX_X, ALU.add))
            link(nc.vector.tensor_scalar(owner[:, 0:PLACES], owner_f[:, :], float(NX - 1), None, ALU.min))
            link(nc.vector.tensor_tensor(first[:, :], end[:, :], nblk[:, :], ALU.subtract))
            link(nc.vector.scalar_tensor_tensor(out=first[:, :], in0=first[:, :], scalar=float(BANK),
                                                in1=counts[:, 0, :], op0=ALU.mult, op1=ALU.add))
            link(nc.vector.tensor_tensor(upto[:, :, :], upto[:, :, :], chosen[:, :, :], ALU.subtract))
            link(nc.vector.tensor_tensor(upto[:, :, :], upto[:, :, :], first[:, :].unsqueeze(1).broadcast_to(wide),
                                         ALU.add))
            for k, one in enumerate((one1, one2)):
                link(nc.vector.tensor_tensor(lg2[:, :, :], one[:, :, :], upto[:, :, :], ALU.mult))
                link(nc.vector.tensor_reduce(r1[:, :], lg2[:, :, :], AX_X, ALU.add))
                link(nc.vector.tensor_copy(place[:, :, k], r1[:, :]))
            dve.wait_ge(route_exp, 1)
            link(nc.vector.tensor_scalar(den[:, :], ex[:, :], 1.0, None, ALU.add))
            link(nc.vector.reciprocal(wtop[:, :, 0], den[:, :]))
            dve.wait_ge(bproj_added, BLOCKS)
            nc.vector.tensor_tensor(wtop[:, :, 1], ex[:, :], wtop[:, :, 0], ALU.mult).then_inc(route, 1)
            dve.wait_ge(route, 2)
            dve.wait_ge(w_stored, 32)

            nc.vector.tensor_copy(br_rep[:, :, :], brT[:, :].unsqueeze(2).broadcast_to([NB, H, P])).then_inc(rep_made, 1)

            def positions(count, i, g, t):
                dve.wait_ge(misc_psum, count + 1)
                wait_from(dve, skew_out[t], (i * GROUPS + g) * 16)
                nc.vector.tensor_tensor(gst[:, t, :], ps[:, MISC_BANK, :], gbias[:, g * BANK:(g + 1) * BANK],
                                        ALU.add).then_inc(g_staged, 1)

            dve.wait_ge(gb_made, GROUPS)
            def sequence(i, start, heads=True, more=True):
                for j in range(H if heads else LAG):
                    for n, (slot, kind, g, t, ahead) in enumerate(UNITS):
                        if slot == j and kind == "g" and heads and (more or not ahead):
                            positions(len(START) + i * len(UNITS) + n, i + ahead, g, t)
                    h = j - 2
                    if here(i, h, heads, start):
                        dve.wait_ge(prob_made, 2 * (i * H + h + 1))
                        wait_from(dve, norm_made, 2 * (i * H + h - 3))
                        nc.vector.reciprocal(inv[:, h % 4, :], total[:, h % 4, :]).then_inc(inv_made, 1)
                    h = j - 1
                    if here(i, h, heads, start):
                        wait_apart(dve, s_psum, i * H + h + 1, const_made)
                        wait_apart(dve, prob_made, 2 * (i * H + h - 1), const_made)
                        if h >= 0 and h % PER == 0:
                            wait_apart(dve, skew_in[2 * (h // PER)], (i + 1) * 16, const_made)
                            dve.wait_ge(skew_in[2 * (h // PER) + 1], (i + 1) * 16)
                        for t, (a, b) in enumerate(((0, P), (P, 3 * P))):
                            ins = nc.vector.tensor_tensor_reduce(
                                out=logit[:, h % 2, a:b], in0=ps[:, S_BANK[h % 2], a:b], in1=extra[:, h % H, a:b],
                                scale=1.0, scalar=BIG, op0=ALU.add, op1=ALU.min, accum_out=low[:, h % 2, t:t + 1])
                        ins.then_inc(logit_made, 1)
                    h = j - 3
                    if here(i, h, heads, start):
                        dve.wait_ge(pT_psum, i * H + h + 1)
                        wait_from(dve, head_psum, i * PAIRS + (h // 2 - 1))
                        nc.vector.tensor_copy(probT[:, h % 4, :], ps[:, PT_BANK, 0:3 * P]).then_inc(pT_made, 1)
                    if j == LAG - 1 and here(i, -1, heads, start):
                        dve.wait_ge(out_psum, i * PAIRS)
                        x = acc[:, at(2 * (i - 1), 2), :]
                        nc.vector.tensor_tensor(x, ps[:, OUT_BANK, 0:2 * E].rearrange("p (t e) -> p t e", t=2), x,
                                                ALU.add).then_inc(attn_added, 1)
                    if j in (LAG, LAG + 2) and start == HALF and here(i, -1, heads, start):
                        add_rows(i - HALF - 1, (j - LAG) // 2)

            def add_rows(n, k):
                if k == 0:
                    wait_from(dve, fetched, (n + 1) * (PER * TOP * 16))
                    dve.wait_ge(attn_added, n + HALF + 1)
                else:
                    dve.wait_ge(added, TOP * n + 1)
                for t in range(PER):
                    x = acc[:, at(PER * n + t, 1), :].rearrange("p a b -> p (a b)")
                    ins = nc.vector.scalar_tensor_tensor(out=x, in0=yget[:, t, k, :],
                                                         scalar=wtop[:, at(PER * n + t, 1), k], in1=x,
                                                         op0=ALU.mult, op1=ALU.add)
                ins.then_inc(added, 1)

            def low_x(b, u):
                dve.wait_ge(xb_high, b + 1)
                wait_from(dve, hid_psum, (b - 1) * FC)
                nc.vector.tensor_tensor(xb_lo[:, u, :], ps[:, XB_BANK[u], :], xb_hi[:, u, :].bitcast(F32),
                                        ALU.subtract).then_inc(xb_low, 1)

            def block_y(b, u, k):
                dve.wait_ge(y_psum, b + 1)
                wait_from(dve, y_out[u], k * 16)
                nc.vector.tensor_tensor(yrow[:, u, :, :], ps[:, Y_BANK[u], :].rearrange("p (t e) -> p t e", t=PER),
                                        w2b[:, u, FF:ROW2].unsqueeze(1).broadcast_to([P, PER, E]),
                                        ALU.add).then_inc(y_made, 1)

            def experts(b, u, k):
                if not isinstance(b, int) or b + 1 < PLACES:
                    low_x(b + 1, 1 - u)
                if not isinstance(b, int) or b > 0:
                    block_y(b - 1, 1 - u, k if u == 1 else k - 1)

            for s0 in (0, HALF):
                s1 = s0 + HALF
                for n, (kind, g, t) in enumerate(START):
                    if kind == "g":
                        positions(s0 * len(UNITS) + n, s0, g, t)
                sequence(s0, s0)
                with dve.Fori(s0 + 1, s1 - 1) as i:
                    sequence(i, s0)
                sequence(s1 - 1, s0, more=False)
                sequence(s1, s0, heads=False, more=False)
                if s0 == 0:
                    low_x(0, 0)
                    for b in range(3):
                        experts(b, b % 2, b // 2)
                    with dve.Fori(2, PLACES // 2) as m:
                        experts(2 * m - 1, 1, m - 1)
                        experts(2 * m, 0, m)
                    for b in range(PLACES - 2, PLACES):
                        experts(b, b % 2, b // 2)
                    block_y(PLACES - 1, (PLACES - 1) % 2, (PLACES - 1) // 2)
            add_rows(HALF - 1, 0)
            add_rows(HALF - 1, 1)

        @block.tensor
        def _(pe):
            def room(g):
                if g >= RING:
                    pe.wait_ge(prep_high, g - RING + 1)
                    done = SPLITS_BEFORE[g - RING + 1]
                    if done:
                        pe.wait_ge(prep_low, done)
                return g % RING

            pe.wait_ge(const_made, 4)
            pe.wait_ge(w2_in, 16)
            for e in range(NX):
                b = room(FIRST["w2"] + e)
                for c in range(FC):
                    mm = nc.tensor.transpose(ps[:, b, c * P:(c + 1) * P], stage[:, FC * e + c, :], ident[:, :])
                mm.then_inc(prep_made, 1)
            pe.wait_ge(small_in, 112)
            for k, (src, rows, cols) in enumerate(((rw_r, NX, E), (b_r, NB, WIN), (b1_r, NX * FC, P), (bq_r, PAIRS, P),
                                                   (br_r, H, NB))):
                b = room(FIRST["small"] + k)
                nc.tensor.transpose(ps[0:cols, b, 0:rows], src[:, :], ident[0:rows, 0:rows]).then_inc(prep_made, 1)
            pe.wait_ge(attn_in, 80)
            for w, src in (("wq", wq_r), ("wk", wk_r)):
                for k in range(2):
                    b = room(FIRST[w] + k)
                    for n in range(4):
                        mm = nc.tensor.transpose(ps[:, b, n * P:(n + 1) * P], src[:, (4 * k + n) * P:(4 * k + n + 1) * P],
                                                 ident[:, :])
                    mm.then_inc(prep_made, 1)
            for k in range(4):
                b = room(FIRST["wr"] + k)
                for n in range(4):
                    h = 4 * k + n
                    mm = nc.tensor.transpose(ps[0:NB, b, n * P:(n + 1) * P], wr_r[:, h * NB:(h + 1) * NB], ident[:, :])
                mm.then_inc(prep_made, 1)
            b = room(FIRST["brev"])
            pe.wait_ge(prep_high, FIRST["small"] + 2)
            nc.tensor.matmul(ps[0:NB, b, 0:WIN], bT[:, :], flip[:, :], start=True, stop=True).then_inc(prep_made, 1)
            for k in range(2):
                b = room(FIRST["qbias"] + k)
                pe.wait_ge(prep_high, FIRST["wr"])
                for n in range(PAIRS):
                    rows = slice(DQ * k, DQ * k + DQ)
                    mm = nc.tensor.matmul(ps[:, b, n:n + 1], wkT[rows, n, :], bqT[rows, n:n + 1], start=True, stop=True)
                mm.then_inc(prep_made, 1)

            for k in range(4):
                b = room(FIRST["wm"] + k)
                pe.wait_ge(prep_high, FIRST["wr"])
                for n in range(4):
                    pair = 4 * (k // 2) + n
                    rows = slice(DQ * (k % 2), DQ * (k % 2) + DQ)
                    mm = nc.tensor.matmul(ps[:, b, n * P:(n + 1) * P], wqT[rows, pair, :], wkT[rows, pair, :],
                                          start=True, stop=True)
                mm.then_inc(prep_made, 1)
            for k in range(4):
                b = room(FIRST["wg"] + k)
                pe.wait_ge(prep_high, FIRST["brev"] + 1)
                for n in range(4):
                    mm = nc.tensor.matmul(ps[:, b, n * P:(n + 1) * P], wrT[:, 4 * k + n, :], brev[:, :],
                                          start=True, stop=True)
                mm.then_inc(prep_made, 1)

            def turn(k, u):
                pe.wait_ge(xn_made, k + 1)
                wait_from(pe, xnT_made, k - 1)
                for n in range(PER):
                    mm = nc.tensor.transpose(ps[:, XT_BANK[u], n * P:(n + 1) * P], xn[:, u, n, :], ident[:, :])
                mm.then_inc(xnT_psum, 1)

            def router(k):
                pe.wait_ge(xnT_made, k + 1)
                wait_from(pe, lgT_made, k)
                nc.tensor.matmul(ps[0:NX, LGT_BANK, :], rwT[:, :], xnT[:, at(k * BANK, BANK)],
                                 start=True, stop=True).then_inc(lgT_psum, 1)

            def router_back(k):
                wait_apart(pe, lgT_made, k + 1, const_made)
                wait_apart(pe, lg_made, k, const_made)
                for n in range(PER):
                    mm = nc.tensor.transpose(ps[:, LG_BANK, n * NX:(n + 1) * NX], lgT[:, n * P:(n + 1) * P],
                                             ident[0:NX, 0:NX])
                mm.then_inc(lg_psum, 1)

            pe.wait_ge(prep_high, FIRST["small"] + 1)
            turn(0, 0)
            turn(1, 1)
            router(0)
            with pe.Fori(1, BLOCKS // 2) as kk:
                for u in range(2):
                    router_back(2 * kk + (u - 2))
                    turn(2 * kk + u, u)
                    router(2 * kk + (u - 1))
            router_back(BLOCKS - 2)
            router(BLOCKS - 1)
            router_back(BLOCKS - 1)

            pe.wait_ge(w1_in, 16)
            for e in range(NX):
                b = room(FIRST["w1"] + e)
                for c in range(FC):
                    mm = nc.tensor.transpose(ps[:, b, c * P:(c + 1) * P], stage[:, FC * e + c, :], ident[:, :])
                mm.then_inc(prep_made, 1)
            pe.wait_ge(prep_high, PREP_GROUPS)
            pe.wait_ge(prep_low, PREP_SPLITS)

            def product(dst, parts, start=True, stop=True):
                (a_hi, a_lo), (b_hi, b_lo) = parts
                nc.tensor.matmul(dst, a_hi, b_hi, start=start, stop=False)
                nc.tensor.matmul(dst, a_hi, b_lo, start=False, stop=False)
                return nc.tensor.matmul(dst, a_lo, b_hi, start=False, stop=stop)

            pe.wait_ge(tally_made, 1)
            pe.wait_ge(scan_const, 3 + NX)
            nc.tensor.matmul(ps[:, 0, 0:NX], lower[:, :], tally[:, :], start=True, stop=True)
            nc.tensor.matmul(ps[:, 0, NX:2 * NX], ones[:, :], tally[:, :], start=True, stop=True
                             ).then_inc(counts_psum, 1)

            def turn_x(b, u, k):
                pe.wait_ge(rows_in[u], 16 * k + 16)
                wait_from(pe, xb_low, b - 1)
                for t in range(PER):
                    mm = nc.tensor.transpose(ps[:, XB_BANK[u], t * P:(t + 1) * P], placed[:, u, t, :], ident[:, :])
                mm.then_inc(xb_psum, 1)

            def expert_in(b, u, k):
                pe.wait_ge(w1b_in[u], 16 * k + 16)
                pe.wait_ge(xb_low, b + 1)
                for c in range(FC):
                    wait_from(pe, hid_made, (b - 1) * FC + c + 1)
                    f = slice(c * P, (c + 1) * P)
                    product(ps[:, H_BANK[c], :], ((w1b[:, u, f], w1b[:, u, FF + c * P:FF + (c + 1) * P]),
                                                  (xb_hi[:, u, :], xb_lo[:, u, :]))).then_inc(hid_psum, 1)

            def expert_out(b, u, k):
                pe.wait_ge(hid_made, (b + 1) * FC)
                pe.wait_ge(w2b_in[u], 16 * k + 16)
                wait_from(pe, y_made, b - 1)
                for t in range(PER):
                    for c in range(FC):
                        mm = nc.tensor.matmul(ps[:, Y_BANK[u], t * P:(t + 1) * P], hid[:, u, c, t * P:(t + 1) * P],
                                              w2b[:, u, c * P:(c + 1) * P], start=(c == 0), stop=(c == FC - 1))
                mm.then_inc(y_psum, 1)

            def experts(b, u, k):
                if not isinstance(b, int) or b + 1 < PLACES:
                    turn_x(b + 1, 1 - u, k + 1 if u == 1 else k)
                expert_in(b, u, k)
                if not isinstance(b, int) or b > 0:
                    expert_out(b - 1, 1 - u, k if u == 1 else k - 1)

            pe.wait_ge(rep_made, 1)
            for k in range(GROUPS):
                for n in range(PER):
                    mm = nc.tensor.matmul(ps[:, k % 4, n * P:(n + 1) * P], br_rep[:, PER * k + n, :], brev[:, :],
                                          start=True, stop=True)
                mm.then_inc(gb_psum, 1)
            pe.wait_ge(gb_made, GROUPS)
            pe.wait_ge(wv_split, 2)

            def unit(kind, n, tile, values, positions):
                wait_from(pe, val_made, values)
                wait_from(pe, g_staged, positions)
                w_hi, w_lo = (wg_hi, wg_lo) if kind == "g" else (wv_hi, wv_lo)
                rows, cols = slice(tile * P, (tile + 1) * P), slice(n * BANK, (n + 1) * BANK)
                product(ps[:, MISC_BANK, :], ((xg_hi[:, rows], xg_lo[:, rows]),
                                              (w_hi[:, cols], w_lo[:, cols]))).then_inc(misc_psum, 1)

            def sequence(i, start, heads=True, more=True):
                n_v, n_g = 1, len(START) - 1
                for j in range(H if heads else LAG):
                    if heads:
                        if j == 0:
                            pe.wait_ge(xq_made, 2 * i + 2)
                        wait_from(pe, q_made, i * H + j - 1)
                        x = at((i % 2) * T, T)
                        product(ps[:, Q_BANK[j % 2], 0:T], ((wm_hi[:, j, :], wm_lo[:, j, :]),
                                                            (xq_hi[:, x], xq_lo[:, x]))).then_inc(q_psum, 1)
                    for n, (slot, kind, k, t, ahead) in enumerate(UNITS):
                        if slot == j and heads and (more or not ahead):
                            if n == LAST_OWN:
                                pe.wait_ge(xg_made, 2 * i + 4)
                            unit(kind, k, t, i * 4 + n_v, i * G_UNITS + n_g)
                            n_v, n_g = n_v + (kind == "v"), n_g + (kind == "g")
                    h = j - 1
                    if here(i, h, heads, start):
                        pe.wait_ge(q_made, i * H + h + 1)
                        wait_from(pe, logit_made, i * H + h - 1)
                        x0 = i * T if h >= 0 else (i - 1) * T
                        nc.tensor.matmul(ps[:, S_BANK[h % 2], 0:P], qry[:, h % 2, 0:P], xnT[:, at(x0, P)],
                                         start=True, stop=True)
                        nc.tensor.matmul(ps[:, S_BANK[h % 2], P:3 * P], qry[:, h % 2, P:T], xnT[:, at(x0, T)],
                                         start=True, stop=True).then_inc(s_psum, 1)
                    h = j - 3
                    if here(i, h, heads, start):
                        pe.wait_ge(norm_made, 2 * (i * H + h + 1))
                        wait_from(pe, pT_made, i * H + h)
                        for n in range(3):
                            mm = nc.tensor.transpose(ps[:, PT_BANK, n * P:(n + 1) * P],
                                                     prob[:, h % 4, n * P:(n + 1) * P], ident[:, :])
                        mm.then_inc(pT_psum, 1)
                    h = j - 4
                    if here(i, h, heads, start) and h % 2:
                        pair = h // 2
                        if pair == 0:
                            pe.wait_ge(val_made, 4 * i + 2)
                        if pair == PAIRS // 2:
                            pe.wait_ge(val_made, 4 * i + 4)
                        pe.wait_ge(pT_made, i * H + h + 1)
                        wait_from(pe, head_made, i * PAIRS + pair)
                        for s in range(2):
                            q = slice(0, T) if s == 0 else slice(P, T)
                            p = slice(0, T) if s == 0 else slice(T, 3 * P)
                            for n in range(2):
                                hh = h - 1 + n
                                v = hh % H * DQ
                                mm = nc.tensor.matmul(ps[DQ * n:DQ * n + DQ, HEAD_BANK, q],
                                                      val[:, s, v:v + DQ], probT[:, hh % 4, p],
                                                      start=(s == 0), stop=(s == 1), skip_group_check=True)
                        mm.then_inc(head_psum, 1)
                    h = j - 5
                    if here(i, h, heads, start) and h % 2:
                        pair = h // 2
                        pe.wait_ge(head_made, i * PAIRS + (pair + 1))
                        if pair == 0:
                            wait_from(pe, attn_added, i)
                        for t in range(2):
                            mm = nc.tensor.matmul(ps[:, OUT_BANK, t * E:(t + 1) * E],
                                                  headT[:, pair % 2, t * P:(t + 1) * P], wproj[:, pair % PAIRS, :],
                                                  start=(pair == 0 and t == 0), stop=(pair == -1),
                                                  skip_group_check=True)
                        mm.then_inc(out_psum, 1)

            for s0 in (0, HALF):
                s1 = s0 + HALF
                pe.wait_ge(xg_made, 2 * s0 + 2)
                for n, (kind, k, t) in enumerate(START):
                    unit(kind, k, t, s0 * 4, s0 * G_UNITS + n)
                sequence(s0, s0)
                with pe.Fori(s0 + 1, s1 - 1) as i:
                    sequence(i, s0)
                sequence(s1 - 1, s0, more=False)
                sequence(s1, s0, heads=False, more=False)
                if s0 == 0:
                    turn_x(0, 0, 0)
                    for b in range(3):
                        experts(b, b % 2, b // 2)
                    with pe.Fori(2, PLACES // 2) as m:
                        experts(2 * m - 1, 1, m - 1)
                        experts(2 * m, 0, m)
                    for b in range(PLACES - 2, PLACES):
                        experts(b, b % 2, b // 2)
                    expert_out(PLACES - 1, (PLACES - 1) % 2, (PLACES - 1) // 2)


_INS = ['L0_attn_X', 'L0_attn_Wq', 'L0_attn_bq', 'L0_attn_Wk', 'L0_attn_Wv', 'L0_attn_Wproj', 'L0_attn_bproj',
        'L0_attn_Wr', 'L0_attn_br', 'L0_attn_b_nd', 'L0_ffn_router_w', 'L0_ffn_w1', 'L0_ffn_b1', 'L0_ffn_w2', 'L0_ffn_b2']
_OUTS = [((32, 256, 128), 'float32')]


def kernel(**inputs):
    import numpy as _np
    import concourse.bacc as _bacc
    from concourse import mybir as _mybir
    from concourse.bass_utils import run_bass_kernel_spmd as _run

    nc = _bacc.Bacc("TRN2", target_bir_lowering=False, num_devices=1)
    arrays, args = {}, []
    for name in _INS:
        a = _np.ascontiguousarray(inputs[name])
        arrays[f"in_{name}_dram"] = a
        args.append(nc.dram_tensor(f"in_{name}_dram", a.shape, _mybir.dt.from_np(a.dtype), kind="ExternalInput").ap())
    for i, (shape, dtype) in enumerate(_OUTS):
        dt = _mybir.dt.from_np(_np.dtype(dtype))
        args.append(nc.dram_tensor(f"out_{i}_dram", shape, dt, kind="ExternalOutput").ap())
    build(nc, *args)
    r = _run(nc, [arrays], core_ids=[0])
    got = tuple(r.results[0][f"out_{i}_dram"] for i in range(len(_OUTS)))
    return got[0]
```
